# Optimizing a Trainium2 kernel written in Bass

```python
import numpy as np
import jax
import jax.numpy as jnp

def _softmax(x, axis=-1):
    return jax.nn.softmax(x, axis=axis)

def _gelu(x):
    return jax.nn.gelu(x, approximate=True)

def _silu(x):
    return jax.nn.silu(x)

def _sigmoid(x):
    return jax.nn.sigmoid(x)

def _layernorm(x, axis=-1, eps=1e-05):
    m = jnp.mean(x, axis=axis, keepdims=True)
    v = jnp.var(x, axis=axis, keepdims=True)
    return (x - m) / jnp.sqrt(v + eps)

def _scatter_add(tgt, idx, src, axis=0):
    return tgt.at[idx].add(src)

def _segment_sum(src, seg, n):
    return jax.ops.segment_sum(src, seg, n)
kernel_name = 'mk_vit_tower_cls_d1_tok_img1024_r4_31c033'

def setup_inputs(seed: int=0):
    np.random.seed(seed)
    _w = jnp.asarray

    def _rec_inputs():
        import jax
        import jax.numpy as jnp
        _rk = jax.random.key(seed)
        x = -0.00016672 + 0.999947 * jax.random.normal(jax.random.fold_in(_rk, 1), (64, 3, 96, 96), jnp.float32)
        cls_tok = 0.02 * jax.random.normal(jax.random.fold_in(_rk, 5), (1, 1, 256), jnp.float32)
        return (x, cls_tok)
    x, cls_tok = _rec_inputs()

    def _L0_tok_setup():
        import jax, jax.numpy as jnp
        import numpy as np
        IMAGE_SIZE = 96
        PATCH = 16
        N_EMBD = 256
        C = 3
        N_PATCHES = (IMAGE_SIZE // PATCH) ** 2
        PATCH_DIM = C * PATCH * PATCH
        key = jax.random.key(seed)
        kx, kw, kb, kp = jax.random.split(key, 4)
        B = 64
        x = jax.random.normal(kx, (B, C, IMAGE_SIZE, IMAGE_SIZE), dtype=jnp.float32)
        bound = 1.0 / np.sqrt(PATCH_DIM)
        W = jax.random.uniform(kw, (N_EMBD, PATCH_DIM), minval=-bound, maxval=bound, dtype=jnp.float32)
        b = jax.random.uniform(kb, (N_EMBD,), minval=-bound, maxval=bound, dtype=jnp.float32)
        pos_embd = jax.random.normal(kp, (1, N_PATCHES, N_EMBD), dtype=jnp.float32) * 0.02
        return {'x': x, 'W': W, 'b': b, 'pos_embd': pos_embd}
    _L0_tok_all = _L0_tok_setup()
    _L0_tok_in = {k: v for k, v in _L0_tok_all.items() if k in ('W', 'b', 'pos_embd')}
    del _L0_tok_all

    def _L0_attn_setup():
        import jax, jax.numpy as jnp
        import numpy as np
        EMB = 256
        HEADS = 16
        ATT = EMB // HEADS
        key = jax.random.key(seed)
        ks = jax.random.split(key, 5)
        s = 1.0 / np.sqrt(EMB)
        return {'x': jax.random.normal(ks[0], (4, 512, EMB), dtype=jnp.float32), 'Wq': jax.random.uniform(ks[1], (EMB, HEADS * ATT), jnp.float32, -s, s), 'Wk': jax.random.uniform(ks[2], (EMB, HEADS * ATT), jnp.float32, -s, s), 'Wv': jax.random.uniform(ks[3], (EMB, HEADS * ATT), jnp.float32, -s, s), 'Wo': jax.random.uniform(ks[4], (HEADS * ATT, EMB), jnp.float32, -s, s)}
    _L0_attn_all = _L0_attn_setup()
    _L0_attn_in = {k: v for k, v in _L0_attn_all.items() if k in ('Wq', 'Wk', 'Wv', 'Wo')}
    del _L0_attn_all

    def _L0_ffn_setup():
        import jax, jax.numpy as jnp
        import numpy as np
        DIM = 256
        INTER = 128
        E = 16
        TOPK = 4
        N_GROUPS = 4
        TOPK_GROUPS = 2
        ROUTE_SCALE = 1.0
        INIT_STD = 0.02
        B, S = (2, 256)
        key = jax.random.key(seed)
        ks = jax.random.split(key, 8)
        return {'x': jax.random.normal(ks[0], (B, S, DIM), jnp.float32), 'gate_w': jax.random.normal(ks[1], (E, DIM), jnp.float32) * INIT_STD, 'gate_bias': jnp.zeros((E,), jnp.float32), 'w1': jax.random.normal(ks[2], (E, INTER, DIM), jnp.float32) * INIT_STD, 'w2': jax.random.normal(ks[3], (E, DIM, INTER), jnp.float32) * INIT_STD, 'w3': jax.random.normal(ks[4], (E, INTER, DIM), jnp.float32) * INIT_STD, 'ws1': jax.random.normal(ks[5], (INTER, DIM), jnp.float32) * INIT_STD, 'ws2': jax.random.normal(ks[6], (DIM, INTER), jnp.float32) * INIT_STD, 'ws3': jax.random.normal(ks[7], (INTER, DIM), jnp.float32) * INIT_STD}
    _L0_ffn_all = _L0_ffn_setup()
    _L0_ffn_in = {k: v for k, v in _L0_ffn_all.items() if k in ('gate_w', 'gate_bias', 'w1', 'w2', 'w3', 'ws1', 'ws2', 'ws3')}
    del _L0_ffn_all
    return {'x': x, 'cls_tok': cls_tok, 'L0_tok_W': _L0_tok_in['W'], 'L0_tok_b': _L0_tok_in['b'], 'L0_tok_pos_embd': _L0_tok_in['pos_embd'], 'L0_attn_Wq': _L0_attn_in['Wq'], 'L0_attn_Wk': _L0_attn_in['Wk'], 'L0_attn_Wv': _L0_attn_in['Wv'], 'L0_attn_Wo': _L0_attn_in['Wo'], 'L0_ffn_gate_w': _L0_ffn_in['gate_w'], 'L0_ffn_gate_bias': _L0_ffn_in['gate_bias'], 'L0_ffn_w1': _L0_ffn_in['w1'], 'L0_ffn_w2': _L0_ffn_in['w2'], 'L0_ffn_w3': _L0_ffn_in['w3'], 'L0_ffn_ws1': _L0_ffn_in['ws1'], 'L0_ffn_ws2': _L0_ffn_in['ws2'], 'L0_ffn_ws3': _L0_ffn_in['ws3']}

def reference(x, cls_tok, L0_tok_W, L0_tok_b, L0_tok_pos_embd, L0_attn_Wq, L0_attn_Wk, L0_attn_Wv, L0_attn_Wo, L0_ffn_gate_w, L0_ffn_gate_bias, L0_ffn_w1, L0_ffn_w2, L0_ffn_w3, L0_ffn_ws1, L0_ffn_ws2, L0_ffn_ws3):
    import jax
    import jax.numpy as jnp

    def _L0_tok_ref(x, W, b, pos_embd):
        import jax, jax.numpy as jnp
        import numpy as np
        IMAGE_SIZE = 96
        PATCH = 16
        N_EMBD = 256
        C = 3
        N_PATCHES = (IMAGE_SIZE // PATCH) ** 2
        PATCH_DIM = C * PATCH * PATCH
        B, Cc, H, Wd = x.shape
        p = PATCH
        Hp, Wp = (H // p, Wd // p)
        patches = x.reshape(B, Cc, Hp, p, Wp, p)
        patches = patches.transpose(0, 2, 4, 1, 3, 5)
        patches = patches.reshape(B, Hp * Wp, Cc * p * p)
        out = jnp.einsum('bnd,ed->bne', patches, W) + b + pos_embd
        return out

    def _L0_attn_ref(x, Wq, Wk, Wv, Wo):
        import jax, jax.numpy as jnp
        import numpy as np
        EMB = 256
        HEADS = 16
        ATT = EMB // HEADS
        b, t, _ = x.shape
        h, d = (HEADS, ATT)
        scale = d ** (-0.25)
        q = (x @ Wq).reshape(b, t, h, d) * scale
        k = (x @ Wk).reshape(b, t, h, d) * scale
        v = (x @ Wv).reshape(b, t, h, d)
        dot = jnp.einsum('bqhd,bkhd->bhqk', q, k)
        causal = jnp.tril(jnp.ones((t, t), dtype=bool))
        dot = jnp.where(causal[None, None], dot, -jnp.inf)
        attn = jax.nn.softmax(dot, axis=-1)
        out = jnp.einsum('bhqk,bkhd->bqhd', attn, v).reshape(b, t, h * d)
        return out @ Wo

    def _L0_ffn_ref(x, gate_w, gate_bias, w1, w2, w3, ws1, ws2, ws3):
        import jax, jax.numpy as jnp
        import numpy as np
        DIM = 256
        INTER = 128
        E = 16
        TOPK = 4
        N_GROUPS = 4
        TOPK_GROUPS = 2
        ROUTE_SCALE = 1.0
        INIT_STD = 0.02
        B, S = (2, 256)
        Bx, Sx, D = x.shape
        T = Bx * Sx
        xf = x.reshape(T, D)
        scores = jax.nn.sigmoid(xf @ gate_w.T)
        original_scores = scores
        s = scores + gate_bias
        sg = s.reshape(T, N_GROUPS, E // N_GROUPS)
        group_scores = sg.max(axis=-1)
        _, gidx = jax.lax.top_k(group_scores, TOPK_GROUPS)
        keep = jnp.zeros((T, N_GROUPS), bool).at[jnp.arange(T)[:, None], gidx].set(True)
        s_masked = jnp.where(keep[:, :, None], sg, -jnp.inf).reshape(T, E)
        _, idx = jax.lax.top_k(s_masked, TOPK)
        weights = jnp.take_along_axis(original_scores, idx, axis=1) * ROUTE_SCALE
        comb = jnp.zeros((T, E), x.dtype).at[jnp.arange(T)[:, None], idx].add(weights)
        h1 = jnp.einsum('td,eid->tei', xf, w1)
        h3 = jnp.einsum('td,eid->tei', xf, w3)
        h = jax.nn.silu(h1) * h3
        y = jnp.einsum('tei,edi,te->td', h, w2, comb)
        z = jax.nn.silu(xf @ ws1.T) * (xf @ ws3.T) @ ws2.T
        return (y + z).reshape(Bx, Sx, D)
    h = _L0_tok_ref(x, L0_tok_W, L0_tok_b, L0_tok_pos_embd)
    h = jnp.concatenate([jnp.broadcast_to(cls_tok, (h.shape[0], 1, h.shape[2])), h], axis=1)
    h = h + _L0_attn_ref(_layernorm(h, axis=-1), L0_attn_Wq, L0_attn_Wk, L0_attn_Wv, L0_attn_Wo)
    h = h + _L0_ffn_ref(_layernorm(h, axis=-1), L0_ffn_gate_w, L0_ffn_gate_bias, L0_ffn_w1, L0_ffn_w2, L0_ffn_w3, L0_ffn_ws1, L0_ffn_ws2, L0_ffn_ws3)
    return h

_drawn_inputs = setup_inputs


def setup_inputs(seed=0):
    import zlib

    import numpy as np

    out = dict(_drawn_inputs(seed))
    spreads = {'L0_ffn_gate_bias': (0.0, 1.299)}
    factors = {'L0_ffn_gate_w': 25.277, 'L0_ffn_ws1': 2.84, 'L0_ffn_ws2': 2.797, 'L0_ffn_ws3': 2.787}
    for name, (base, spread) in spreads.items():
        noise = np.random.default_rng([zlib.crc32(name.encode()), seed]).standard_normal(out[name].shape)
        drawn = base * np.exp(spread * noise) if base else spread * noise
        out[name] = jnp.asarray(drawn.astype(out[name].dtype))
    for name, factor in factors.items():
        out[name] = (out[name] * factor).astype(out[name].dtype)
    return out
```

```python
from contextlib import ExitStack

import numpy as np

import concourse.bass as bass
from concourse import mybir

ALU = mybir.AluOpType
ACT = mybir.ActivationFunctionType
AX = mybir.AxisListType
F32 = mybir.dt.float32
BF16 = mybir.dt.bfloat16

P = 128
B, N, D = 64, 37, 256
HEADS, HD = 16, 16
PC = 6
E, TOPK = 16, 4
GROUPS, TOPG = 4, 2
ITERS = 4
IMGS = B // ITERS
TOK = IMGS * N
TILES = -(-TOK // P)
ROWS = [min(P, TOK - P * t) for t in range(TILES)]
PAIRS = IMGS // 2
CH = TOK // 2
HG = 8
NE = E + 1
EPS = 1e-5
NEG = -1e30
SPAN = 64 + N


def build(nc, xT, wpT, pos, bias, wqkvo, gateT, gbias, w13, w2, ident, causal, hmask, vmask,
          below, sel, out):
    with ExitStack() as ctx:
        def sb(name, shape, dt=F32):
            return ctx.enter_context(nc.sbuf_tensor(name, shape, dt))

        def sem(name):
            return ctx.enter_context(nc.semaphore(name))

        wp_s = sb("wp_s", [P, PC, D])
        tab = sb("tab", [P, TILES, D])

        w_s = sb("w_s", [P, 4, 2, D])
        gate_s = sb("gate_s", [P, 2, E])
        gb_s = sb("gb_s", [P, TILES, E])
        w13_s = sb("w13_s", [P, NE, 2, 2, P])
        w2_s = sb("w2_s", [P, NE, D])
        id_s = sb("id_s", [P, P])
        idb_s = sb("idb_s", [P, P], BF16)
        causal_s = sb("causal_s", [P, HG, N], BF16)
        hmask_s = sb("hmask_s", [P, HG])
        vmask_s = sb("vmask_s", [2 * N, D])
        below_s = sb("below_s", [P, E, E])
        sel_s = sb("sel_s", [96, E, P], BF16)
        half_s = sb("half_s", [P, 1])
        eps_s = sb("eps_s", [P, 1])
        x_s = sb("x_s", [P, PC, TOK])
        h_nat = sb("h_nat", [P, TILES, D])
        xn = sb("xn", [P, TILES, D])
        h2 = sb("h2", [P, TILES, D])
        hnT = sb("hnT", [P, 2, TOK])
        hdup = sb("hdup", [P, 2, IMGS, 2, N])
        st = sb("st", [P, 2, TILES, 6])
        mv = sb("mv", [P, 2, TILES, 2])
        ve = sb("ve", [P, 2, TILES])
        rstd = sb("rstd", [P, 2, TILES])
        qT = sb("qT", [P, 2, IMGS, N])
        kT = sb("kT", [P, 2, IMGS, N])
        work = sb("work", [P, 8 * HG * N + 2 * HEADS * N])
        bdk = work[:, 0:8 * HG * N].rearrange("p (b g m n) -> p b g m n", b=2, g=2, m=2)
        ex = work[:, 8 * HG * N:].rearrange("p (b h k) -> p b h k", b=2, h=HEADS)
        sel_f = work[0:96, 0:E * P].rearrange("p (e q) -> p e q", e=E)
        causal_f = work[:, E * P:E * P + HG * N].rearrange("p (h k) -> p h k", h=HG)
        ecmp = work[:, 0:2 * TILES * E * E].rearrange("p (s t e f) -> p s t e f", s=2, t=TILES, e=E)
        bdv = sb("bdv", [2 * N, IMGS, D])
        nmax = sb("nmax", [P, 2, HEADS])
        rsum = sb("rsum", [P, 2, HEADS])
        rinv = sb("rinv", [P, 2, HEADS])

        pn = sb("pn", [P, 2, HEADS, N])
        ptT = sb("ptT", [2 * N, 2, 8, 2, N])
        oT = sb("oT", [P, 2, TOK])
        rT = sb("rT", [P, 4, TOK])
        lg = sb("lg", [P, TILES, E])
        lg1 = sb("lg1", [P, TILES, E])
        sc = sb("sc", [P, TILES, E])
        biased = sb("biased", [P, TILES, E])
        gmax = sb("gmax", [P, TILES, GROUPS])
        gcmp = sb("gcmp", [P, 2, TILES, GROUPS, GROUPS])
        grank = sb("grank", [P, TILES, GROUPS])
        keep = sb("keep", [P, TILES, GROUPS])
        kneg = sb("kneg", [P, TILES, GROUPS])
        sm = sb("sm", [P, TILES, E])
        rank = sb("rank", [P, TILES, E])
        comb = sb("comb", [P, 3, TILES, E])
        combp = sb("combp", [P, TILES, 3, 32], BF16)
        combT = sb("combT", [96, TOK], BF16)
        sil = sb("sil", [P, 2, CH])
        us = sb("us", [P, 2, CH])
        gs = sb("gs", [P, 2, CH])
        yo = sb("yo", [P, 2, 2, CH])

        bank = [ctx.enter_context(nc.psum_tensor(f"bank{b}", [P, 512], F32)) for b in range(6)]
        bankO = ctx.enter_context(nc.psum_tensor("bankO", [P, 512], F32))
        bankG = ctx.enter_context(nc.psum_tensor("bankG", [P, 512], F32))

        names = """x_in w_in moe_in tab_sum init
        dup_ok patched h_ok h_stat h_agg h_var h_rstd xn_ok xT_ps hnT_ok qk_ps qk_ok v_ps bdv_ok
        bdk0 bdk1 s_ps s_max s_sub s_exp s_sum s_inv s_norm pt_ps pt_ok o_ps o_ok
        wo_ps h2_ok h2_stat h2_agg h2_var h2_rstd x2_ok t2_ps t2_ok lg_ps lg_exp route_step comb_ok ct_ps ct_ok
        up_ps sil_ok u_ok g_ok cb_ps y_ps yo_ok yo_free stored""".split()
        S = {n: sem(n) for n in names}
        block = ctx.enter_context(nc.Block())
        CONST_LOADS = 12
        INITS = 11
        ROUTE_STEPS = 23

        def tile(t):
            return slice(P * t, P * t + ROWS[t])

        def settled(eng):
            eng.wait_ge(S["w_in"], 16 * CONST_LOADS)

        def CB(r):
            return (bankG if r % 2 else bankO)[:, 0:CH]

        def CT(t):
            return (bankG if t % 2 else bankO)[0:96, :].bitcast(BF16)[:, 0:ROWS[t]]

        @block.sync
        def _(sp):
            for dst, src in ((wp_s, wpT), (tab, pos), (h2, bias), (w_s, wqkvo), (id_s, ident),
                             (causal_f, causal), (hmask_s, hmask), (vmask_s, vmask), (gate_s, gateT),
                             (gb_s, gbias), (below_s, below), (sel_f, sel)):
                dst = dst if dst is causal_f or dst is sel_f else dst[:]
                sp.dma_start(dst, src).then_inc(S["w_in"], 16)
            sp.dma_start(x_s[:], xT[0]).then_inc(S["x_in"], 16)
            sp.dma_start(w13_s[:], w13).then_inc(S["moe_in"], 16)
            sp.dma_start(w2_s[:], w2).then_inc(S["moe_in"], 16)

            def store(i):
                for c in range(2):
                    sp.wait_ge(S["yo_ok"], i * 4 + 2 * c + 2)
                    sp.dma_start(out[:, :, bass.ds(i * TOK + c * CH, CH)], yo[:, c]).then_inc(S["stored"], 16)

            sp.sem_inc(S["yo_free"], 1)
            with sp.Fori(0, ITERS - 1) as i:
                sp.wait_ge(S["patched"], (i + 1) * TILES)
                sp.dma_start(x_s[:], xT[bass.ds(i + 1, 1)].rearrange("i p c t -> p (i c) t")).then_inc(S["x_in"], 16)
                store(i)
                sp.wait_ge(S["stored"], (i + 1) * 32)
                sp.sem_inc(S["yo_free"], 1)
            store(ITERS - 1)
            sp.wait_ge(S["stored"], 16 * 2 * ITERS)

        @block.gpsimd
        def _(pool):
            pool.memset(half_s[:], -0.5).then_inc(S["init"], 1)
            pool.memset(eps_s[:], EPS).then_inc(S["init"], 1)
            pool.memset(combp[:], 0.0).then_inc(S["init"], 1)
            pool.wait_ge(S["init"], INITS)
            pool.wait_ge(S["w_in"], 16 * CONST_LOADS)

            def rstds(i, which, agg, var, done):
                for t in range(TILES):
                    r = ROWS[t]
                    pool.wait_ge(S[agg], i * TILES + t + 1)
                    pool.tensor_tensor(ve[0:r, which, t:t + 1], mv[0:r, which, t, 1:2], eps_s[0:r],
                                       ALU.add).then_inc(S[var], 1)
                    pool.wait_ge(S[var], i * TILES + t + 1)
                    pool.tensor_tensor(rstd[0:r, which, t:t + 1], ve[0:r, which, t:t + 1], half_s[0:r],
                                       ALU.pow).then_inc(S[done], 1)

            with pool.Fori(0, ITERS) as i:
                rstds(i, 0, "h_agg", "h_var", "h_rstd")
                for p in range(PAIRS + 1):
                    if p < PAIRS:
                        if p == 0:
                            pool.wait_ge(S["qk_ok"], i * 8 + 8)
                        if p >= 2:
                            pool.wait_ge(S["s_ps"], i * PAIRS + p - 1)
                        pool.tensor_tensor(
                            bdk[:, p % 2, 1].rearrange("p m (h k) -> p m h k", h=HG),
                            kT[:, 1, 2 * p:2 * p + 2, None, :].to_broadcast([P, 2, HG, N]),
                            hmask_s[:, None, :, None].to_broadcast([P, 2, HG, N]),
                            ALU.mult).then_inc(S["bdk1"], 1)
                    if p >= 1:
                        q = p - 1
                        pool.wait_ge(S["s_inv"], i * PAIRS + q + 1)
                        if q >= 2:
                            pool.wait_ge(S["pt_ps"], i * PAIRS + q - 1)
                        pool.tensor_tensor(pn[0:SPAN, q % 2], ex[0:SPAN, q % 2],
                                           rinv[0:SPAN, q % 2, :, None].to_broadcast([SPAN, HEADS, N]),
                                           ALU.mult).then_inc(S["s_norm"], 1)
                rstds(i, 1, "h2_agg", "h2_var", "h2_rstd")

        @block.scalar
        def _(act):
            with act.Fori(0, ITERS) as i:
                for t in range(TILES):
                    act.wait_ge(S["xT_ps"], i * TILES + t + 1)
                    act.activation(hnT[:, :, tile(t)],
                                   bank[2 + t % 2][:, 0:2 * P].rearrange("p (c t) -> p c t", c=2)[:, :, 0:ROWS[t]],
                                   ACT.Copy).then_inc(S["hnT_ok"], 1)
                for n in range(8):
                    half, g, is_k = n // 4, n // 2 % 2, n % 2
                    act.wait_ge(S["qk_ps"], i * 8 + n + 1)
                    dst = (kT if is_k else qT)[:, g, half * IMGS // 2:(half + 1) * IMGS // 2, :]
                    act.activation(dst, bank[n % 4][:, 0:CH].rearrange("p (m t) -> p m t", t=N), ACT.Copy,
                                   scale=1.0 if is_k else HD ** -0.5).then_inc(S["qk_ok"], 1)

                def pt_out(p):
                    act.wait_ge(S["pt_ps"], i * PAIRS + p + 1)
                    if p >= 2:
                        act.wait_ge(S["o_ps"], i * PAIRS + p - 1)
                    for hf in range(2):
                        a = act.activation(
                            ptT[:, p % 2, 4 * hf:4 * hf + 4].rearrange("p c m t -> p c m t"),
                            bank[4 + hf][0:2 * N, :].rearrange("p (c m t) -> p c m t", c=4, m=2)[:, :, :, 0:N],
                            ACT.Copy)
                    a.then_inc(S["pt_ok"], 1)

                for p in range(PAIRS + 1):
                    if p < PAIRS:
                        act.wait_ge(S["s_sub"], i * PAIRS + p + 1)
                        act.activation(ex[0:SPAN, p % 2], ex[0:SPAN, p % 2], ACT.Exp).then_inc(S["s_exp"], 1)
                    if p >= 1:
                        pt_out(p - 1)
                for t in range(TILES):
                    act.wait_ge(S["t2_ps"], i * TILES + t + 1)
                    act.activation(rT[:, :, tile(t)],
                                   bank[2 + t % 2][:].rearrange("p (c t) -> p c t", c=4)[:, :, 0:ROWS[t]],
                                   ACT.Copy).then_inc(S["t2_ok"], 1)
                act.wait_ge(S["lg_ps"], i + 1)
                act.activation(lg[:], bankG[:, 0:TILES * E].rearrange("p (t e) -> p t e", e=E), ACT.Exp,
                               scale=-1.0).then_inc(S["lg_exp"], 1)
                for k in range(2 * NE):
                    act.wait_ge(S["up_ps"], i * 2 * NE + k + 1)
                    if k >= 2:
                        act.wait_ge(S["g_ok"], i * 2 * NE + k - 1)
                    act.activation(sil[:, k % 2], bank[2 * (k % 2)][:, 0:CH], ACT.Silu).then_inc(S["sil_ok"], 1)

        @block.vector
        def _(dve):
            for b in bank[0:4] + [bankG]:
                dve.memset(b[:], 0.0).then_inc(S["init"], 1)
            dve.wait_ge(S["w_in"], 16 * CONST_LOADS)
            for dst, src in ((idb_s[:], id_s[:]), (sel_s[:], sel_f), (causal_s[:], causal_f)):
                dve.tensor_copy(dst, src).then_inc(S["init"], 1)
            dve.tensor_tensor(tab[:], tab[:], h2[:], ALU.add).then_inc(S["tab_sum"], 1)
            dve.wait_ge(S["tab_sum"], 1)

            def layernorm(i, which, ps, other, res, pre, done, store):
                for t in range(TILES + 1):
                    if t < TILES:
                        r = ROWS[t]
                        dve.wait_ge(S[ps], i * TILES + t + 1)
                        dve.tensor_tensor(res[0:r, t], bank[t % 2][0:r, 0:D], other[0:r, t],
                                          ALU.add).then_inc(S[pre + "_ok"], 1)
                        dve.wait_ge(S[pre + "_ok"], i * TILES + t + 1)
                        dve.bn_stats(st[0:r, which, t], res[0:r, t]).then_inc(S[pre + "_stat"], 1)
                        settled(dve)
                        dve.wait_ge(S[pre + "_stat"], i * TILES + t + 1)
                        dve.bn_aggr(mv[0:r, which, t], st[0:r, which, t]).then_inc(S[pre + "_agg"], 1)
                    if t >= 1:
                        q, r = t - 1, ROWS[t - 1]
                        dve.wait_ge(S[pre + "_agg"], i * TILES + q + 1)
                        dve.wait_ge(S[pre + "_rstd"], i * TILES + q + 1)
                        dve.tensor_scalar(store[0:r, q], res[0:r, q], mv[0:r, which, q, 0:1],
                                          rstd[0:r, which, q:q + 1], ALU.subtract, ALU.mult).then_inc(S[done], 1)

            with dve.Fori(0, ITERS) as i:
                layernorm(i, 0, "patched", tab, h_nat, "h", "xn_ok", xn)
                dve.wait_ge(S["hnT_ok"], (i + 1) * TILES)
                for c in range(2):
                    dve.tensor_copy(hdup[:, c], hnT[:, c].rearrange("p (m t) -> p m t", t=N)[:, :, None, :]
                                    .to_broadcast([P, IMGS, 2, N])).then_inc(S["dup_ok"], 1)
                for m in range(IMGS):
                    dve.wait_ge(S["v_ps"], i * IMGS + m + 1)
                    dve.tensor_tensor(bdv[:, m], bank[m % 4][0:2 * N, 0:D], vmask_s[:],
                                      ALU.mult).then_inc(S["bdv_ok"], 1)

                def heads_apart(p):
                    if p == 0:
                        dve.wait_ge(S["qk_ok"], i * 8 + 8)
                    if p >= 2:
                        dve.wait_ge(S["s_ps"], i * PAIRS + p - 1)
                    dve.tensor_tensor(
                        bdk[:, p % 2, 0].rearrange("p m (h k) -> p m h k", h=HG),
                        kT[:, 0, 2 * p:2 * p + 2, None, :].to_broadcast([P, 2, HG, N]),
                        hmask_s[:, None, :, None].to_broadcast([P, 2, HG, N]),
                        ALU.mult).then_inc(S["bdk0"], 1)

                def max_sub(p):
                    dve.wait_ge(S["s_ps"], i * PAIRS + p + 1)
                    for g in range(2):
                        sg = bank[2 * (p % 2) + g][0:SPAN, 0:HG * N].rearrange("p (h k) -> p h k", h=HG)
                        a = dve.tensor_reduce(nmax[0:SPAN, p % 2, HG * g:HG * g + HG], sg, AX.X, ALU.max,
                                              negate=True)
                    a.then_inc(S["s_max"], 1)
                    dve.wait_ge(S["s_max"], i * PAIRS + p + 1)
                    for g in range(2):
                        sg = bank[2 * (p % 2) + g][0:SPAN, 0:HG * N].rearrange("p (h k) -> p h k", h=HG)
                        a = dve.tensor_tensor(
                            ex[0:SPAN, p % 2, HG * g:HG * g + HG], sg,
                            nmax[0:SPAN, p % 2, HG * g:HG * g + HG, None].to_broadcast([SPAN, HG, N]), ALU.add)
                    a.then_inc(S["s_sub"], 1)

                def sums(p):
                    dve.wait_ge(S["s_exp"], i * PAIRS + p + 1)
                    dve.tensor_reduce(rsum[0:SPAN, p % 2], ex[0:SPAN, p % 2], AX.X, ALU.add).then_inc(S["s_sum"], 1)
                    dve.wait_ge(S["s_sum"], i * PAIRS + p + 1)
                    dve.reciprocal(rinv[0:SPAN, p % 2], rsum[0:SPAN, p % 2]).then_inc(S["s_inv"], 1)

                def o_out(p):
                    dve.wait_ge(S["o_ps"], i * PAIRS + p + 1)
                    dve.tensor_copy(oT[:, :, 2 * N * p:2 * N * (p + 1)],
                                    bankO[:, 0:4 * N].rearrange("p (g t) -> p g t", g=2)).then_inc(S["o_ok"], 1)

                heads_apart(0)
                for p in range(PAIRS + 2):
                    if p + 1 < PAIRS:
                        heads_apart(p + 1)
                    if p < PAIRS:
                        max_sub(p)
                        sums(p)
                    if p >= 2:
                        o_out(p - 2)

                layernorm(i, 1, "wo_ps", h_nat, h2, "h2", "x2_ok", xn)

                steps = 0

                def step(ins):
                    nonlocal steps
                    steps += 1
                    ins.then_inc(S["route_step"], 1)
                    dve.wait_ge(S["route_step"], i * ROUTE_STEPS + steps)

                dve.wait_ge(S["lg_exp"], i + 1)
                step(dve.tensor_scalar(lg1[:], lg[:], 1.0, None, ALU.add))
                step(dve.reciprocal(sc[:], lg1[:]))
                step(dve.tensor_tensor(biased[:], sc[:], gb_s[:], ALU.add))
                by_group = biased[:].rearrange("p t (g k) -> p (t g) k", g=GROUPS)
                step(dve.tensor_reduce(gmax[:].rearrange("p t g -> p (t g)"), by_group, AX.X, ALU.max))

                def ranks(val, n, gt, eq, res):
                    mine = val[:, :, :, None].to_broadcast([P, TILES, n, n])
                    other = val[:, :, None, :].to_broadcast([P, TILES, n, n])
                    lower = below_s[:, None, 0:n, 0:n].to_broadcast([P, TILES, n, n])
                    step(dve.tensor_tensor(gt, other, mine, ALU.is_gt))
                    step(dve.tensor_tensor(eq, other, mine, ALU.is_equal))
                    step(dve.tensor_tensor(eq, eq, lower, ALU.mult))
                    step(dve.tensor_tensor(gt, gt, eq, ALU.add))
                    step(dve.tensor_reduce(res, gt, AX.X, ALU.add))

                ranks(gmax, GROUPS, gcmp[:, 0], gcmp[:, 1], grank[:])
                step(dve.tensor_scalar(keep[:], grank[:], float(TOPG), None, ALU.is_lt))
                step(dve.tensor_scalar(kneg[:], keep[:], -1.0, -NEG, ALU.add, ALU.mult))
                masked = sm[:].rearrange("p t (g k) -> p (t g) k", g=GROUPS)
                shape = [P, TILES * GROUPS, E // GROUPS]
                step(dve.tensor_tensor(masked, by_group,
                                       keep[:].rearrange("p t g -> p (t g)")[:, :, None].to_broadcast(shape), ALU.mult))
                step(dve.tensor_tensor(masked, masked,
                                       kneg[:].rearrange("p t g -> p (t g)")[:, :, None].to_broadcast(shape), ALU.add))
                ranks(sm, E, ecmp[:, 0], ecmp[:, 1], rank[:])
                step(dve.scalar_tensor_tensor(comb[:, 0], rank[:], float(TOPK), sc[:], ALU.is_lt, ALU.mult))
                step(dve.tensor_copy(combp[:, :, 0, 0:E], comb[:, 0]))
                step(dve.tensor_tensor(comb[:, 1], comb[:, 0], combp[:, :, 0, 0:E], ALU.subtract))
                step(dve.tensor_copy(combp[:, :, 1, 0:E], comb[:, 1]))
                step(dve.tensor_tensor(comb[:, 2], comb[:, 1], combp[:, :, 1, 0:E], ALU.subtract))
                dve.tensor_copy(combp[:, :, 2, 0:E], comb[:, 2]).then_inc(S["comb_ok"], 1)
                assert steps == ROUTE_STEPS
                for t in range(TILES):
                    dve.wait_ge(S["ct_ps"], i * TILES + t + 1)
                    dve.tensor_copy(combT[:, tile(t)], CT(t)).then_inc(S["ct_ok"], 1)

                for k in range(2 * NE):
                    c, e = divmod(k, NE)
                    dve.wait_ge(S["sil_ok"], i * 2 * NE + k + 1)
                    if k >= 2:
                        dve.wait_ge(S["y_ps"], i * 2 * NE + k - 1)
                    h3 = bank[2 * (k % 2) + 1][:, 0:CH]
                    if e == 0:
                        dve.tensor_tensor(gs[:, k % 2], sil[:, k % 2], h3, ALU.mult).then_inc(S["g_ok"], 1)
                    else:
                        r = c * E + e - 1
                        dve.tensor_tensor(us[:, k % 2], sil[:, k % 2], h3, ALU.mult).then_inc(S["u_ok"], 1)
                        dve.wait_ge(S["u_ok"], i * 2 * E + r + 1)
                        dve.wait_ge(S["cb_ps"], i * 2 * E + r + 1)
                        dve.tensor_tensor(gs[:, k % 2], us[:, k % 2], CB(r), ALU.mult).then_inc(S["g_ok"], 1)
                    if e == NE - 1:
                        dve.wait_ge(S["y_ps"], i * 2 * NE + k + 1)
                        dve.wait_ge(S["yo_free"], i + 1)
                        for d in range(2):
                            a = dve.tensor_tensor(yo[:, c, d], bank[4 + d][:, 0:CH],
                                                  rT[:, d, c * CH:(c + 1) * CH], ALU.add)
                            a.then_inc(S["yo_ok"], 1)

        @block.tensor
        def _(pe):
            pe.wait_ge(S["w_in"], 16 * CONST_LOADS)
            pe.wait_ge(S["init"], INITS)
            with pe.Fori(0, ITERS) as i:
                pe.wait_ge(S["x_in"], i * 16 + 16)
                for t in range(TILES):
                    if t >= 2:
                        pe.wait_ge(S["h_ok"], i * TILES + t - 1)
                    for c in range(PC):
                        m = pe.matmul(bank[t % 2][0:ROWS[t], 0:D], x_s[:, c, tile(t)], wp_s[:, c],
                                      start=(c == 0), stop=(c == PC - 1))
                    m.then_inc(S["patched"], 1)
                for t in range(TILES):
                    pe.wait_ge(S["xn_ok"], i * TILES + t + 1)
                    if t >= 2:
                        pe.wait_ge(S["hnT_ok"], i * TILES + t - 1)
                    for c in range(2):
                        m = pe.transpose(bank[2 + t % 2][:, P * c:P * c + ROWS[t]],
                                         xn[0:ROWS[t], t, P * c:P * c + P], id_s[0:ROWS[t], 0:ROWS[t]])
                    m.then_inc(S["xT_ps"], 1)
                pe.wait_ge(S["hnT_ok"], (i + 1) * TILES)
                for n in range(8):
                    half, g, is_k = n // 4, n // 2 % 2, n % 2
                    if n >= 4:
                        pe.wait_ge(S["qk_ok"], i * 8 + n - 3)
                    for c in range(2):
                        m = pe.matmul(bank[n % 4][:, 0:CH], w_s[:, is_k, c, P * g:P * g + P],
                                      hnT[:, c, CH * half:CH * half + CH], start=(c == 0), stop=(c == 1))
                    m.then_inc(S["qk_ps"], 1)
                pe.wait_ge(S["dup_ok"], (i + 1) * 2)
                for m_ in range(IMGS):
                    if m_ < 4:
                        pe.wait_ge(S["qk_ok"], i * 8 + 5 + m_)
                    else:
                        pe.wait_ge(S["bdv_ok"], i * IMGS + m_ - 3)
                    for c in range(2):
                        keys = hdup[:, c, m_].rearrange("p r t -> p (r t)")
                        m = pe.matmul(bank[m_ % 4][0:2 * N, 0:D], keys, w_s[:, 2, c], start=(c == 0), stop=(c == 1))
                    m.then_inc(S["v_ps"], 1)

                def scores(p):
                    pe.wait_ge(S["bdk0"], i * PAIRS + p + 1)
                    pe.wait_ge(S["bdk1"], i * PAIRS + p + 1)
                    if p < 2:
                        pe.wait_ge(S["bdv_ok"], i * IMGS + 14 + 2 * p)
                    else:
                        pe.wait_ge(S["s_sub"], i * PAIRS + p - 1)
                    for g in range(2):
                        for m_ in range(2):
                            o = bank[2 * (p % 2) + g][64 * m_:64 * m_ + N, 0:HG * N]
                            pe.matmul(o, idb_s[:, 0:N], causal_s[:].rearrange("k h q -> k (h q)"),
                                      start=True, stop=False)
                            m = pe.matmul(o, qT[:, g, 2 * p + m_], bdk[:, p % 2, g, m_], start=False, stop=True)
                    m.then_inc(S["s_ps"], 1)

                def turn(p):
                    pe.wait_ge(S["s_norm"], i * PAIRS + p + 1)
                    if p >= 1:
                        pe.wait_ge(S["pt_ok"], i * PAIRS + p)
                    for c in range(8):
                        m = pe.transpose(bank[4 + c // 4][0:2 * N, P * (c % 4):P * (c % 4) + SPAN],
                                         pn[0:SPAN, p % 2, 2 * c:2 * c + 2].rearrange("p h k -> p (h k)"),
                                         id_s[0:SPAN, 0:SPAN])
                    m.then_inc(S["pt_ps"], 1)

                def values(p):
                    pe.wait_ge(S["pt_ok"], i * PAIRS + p + 1)
                    if p >= 1:
                        pe.wait_ge(S["o_ok"], i * PAIRS + p)
                    for m_ in range(2):
                        for c in range(8):
                            col = 2 * N * (c // 4) + N * m_
                            m = pe.matmul(bankO[32 * (c % 4):32 * (c % 4) + 32, col:col + N],
                                          bdv[:, 2 * p + m_, 32 * c:32 * c + 32], ptT[:, p % 2, c, m_],
                                          start=True, stop=True)
                    m.then_inc(S["o_ps"], 1)

                scores(0)
                for p in range(PAIRS + 1):
                    if p + 1 < PAIRS:
                        scores(p + 1)
                    if p >= 1:
                        values(p - 1)
                    if p < PAIRS:
                        turn(p)
                pe.wait_ge(S["o_ok"], (i + 1) * PAIRS)
                for t in range(TILES):
                    if t >= 2:
                        pe.wait_ge(S["h2_ok"], i * TILES + t - 1)
                    for c in range(2):
                        m = pe.matmul(bank[t % 2][0:ROWS[t], 0:D], oT[:, c, tile(t)], w_s[:, 3, c],
                                      start=(c == 0), stop=(c == 1))
                    m.then_inc(S["wo_ps"], 1)
                for t in range(TILES):
                    pe.wait_ge(S["x2_ok"], i * TILES + t + 1)
                    if t >= 2:
                        pe.wait_ge(S["t2_ok"], i * TILES + t - 1)
                    for c in range(4):
                        src = h2 if c < 2 else xn
                        m = pe.transpose(bank[2 + t % 2][:, P * c:P * c + ROWS[t]],
                                         src[0:ROWS[t], t, P * (c % 2):P * (c % 2) + P],
                                         id_s[0:ROWS[t], 0:ROWS[t]])
                    m.then_inc(S["t2_ps"], 1)
                pe.wait_ge(S["t2_ok"], (i + 1) * TILES)
                for t in range(TILES):
                    for c in range(2):
                        m = pe.matmul(bankG[0:ROWS[t], E * t:E * t + E], rT[:, 2 + c, tile(t)], gate_s[:, c],
                                      start=(c == 0), stop=(c == 1))
                m.then_inc(S["lg_ps"], 1)
                pe.wait_ge(S["comb_ok"], i + 1)
                for t in range(TILES):
                    if t >= 2:
                        pe.wait_ge(S["ct_ok"], i * TILES + t - 1)
                    pe.transpose(CT(t), combp[0:ROWS[t], t].rearrange("p s e -> p (s e)"),
                                 idb_s[0:ROWS[t], 0:ROWS[t]]).then_inc(S["ct_ps"], 1)
                pe.wait_ge(S["ct_ok"], (i + 1) * TILES)
                pe.wait_ge(S["moe_in"], 32)

                def up(k):
                    c, e = divmod(k, NE)
                    if k >= 2:
                        pe.wait_ge(S["g_ok"], i * 2 * NE + k - 1)
                    for w in range(2):
                        for d in range(2):
                            m = pe.matmul(bank[2 * (k % 2) + w][:, 0:CH], w13_s[:, e, w, d],
                                          rT[:, 2 + d, CH * c:CH * c + CH], start=(d == 0), stop=(d == 1))
                    m.then_inc(S["up_ps"], 1)
                    if e > 0:
                        r = c * E + e - 1
                        if r >= 2:
                            pe.wait_ge(S["g_ok"], i * 2 * NE + (r - 2) // E * NE + (r - 2) % E + 2)
                        pe.matmul(CB(r), sel_s[:, e - 1], combT[:, CH * c:CH * c + CH],
                                  start=True, stop=True).then_inc(S["cb_ps"], 1)

                def down(k):
                    c, e = divmod(k, NE)
                    pe.wait_ge(S["g_ok"], i * 2 * NE + k + 1)
                    if k == NE:
                        pe.wait_ge(S["yo_ok"], i * 4 + 2)
                    for d in range(2):
                        m = pe.matmul(bank[4 + d][:, 0:CH], w2_s[:, e, P * d:P * d + P], gs[:, k % 2],
                                      start=(e == 0), stop=(e == NE - 1))
                    m.then_inc(S["y_ps"], 1)

                up(0)
                for k in range(2 * NE):
                    if k + 1 < 2 * NE:
                        up(k + 1)
                    down(k)


def _lay_out(inp):
    def rows(a):
        return np.ascontiguousarray(a.reshape(-1, P, a.shape[-1]).transpose(1, 0, 2))

    def tiled(a):
        full = np.zeros((TILES * P, a.shape[-1]), a.dtype)
        full[:TOK] = a
        return np.ascontiguousarray(full.reshape(TILES, P, -1).transpose(1, 0, 2))

    x = inp["x"]
    G = x.shape[-1] // 16
    patches = x.reshape(B, 3, G, 16, G, 16).transpose(1, 3, 5, 0, 2, 4).reshape(PC * P, B, G * G)
    xT = np.zeros((PC * P, B, N), x.dtype)
    xT[:, :, 1:] = patches
    xT = xT.reshape(PC, P, ITERS, TOK).transpose(2, 1, 0, 3)
    pos = np.concatenate([inp["cls_tok"][0], inp["L0_tok_pos_embd"][0]])
    bias = np.zeros((N, D), x.dtype)
    bias[1:] = inp["L0_tok_b"]
    wqkvo = np.stack([rows(inp["L0_attn_" + n]) for n in ("Wq", "Wk", "Wv", "Wo")], axis=1)
    w1 = np.concatenate([inp["L0_ffn_ws1"][None], inp["L0_ffn_w1"]])
    w3 = np.concatenate([inp["L0_ffn_ws3"][None], inp["L0_ffn_w3"]])
    w2 = np.concatenate([inp["L0_ffn_ws2"][None], inp["L0_ffn_w2"]])
    w13 = np.stack([w1, w3], axis=1).reshape(NE, 2, P, 2, P).transpose(4, 0, 1, 3, 2)
    ch = np.arange(D)
    causal = np.where(np.arange(N)[None, :] > np.arange(P)[:, None], NEG, 0.0)
    causal[N:] = 0.0
    sel = np.zeros((3, 32, E, P))
    for e in range(E):
        sel[:, e, e] = 1.0
    return {
        "xT": xT, "wpT": rows(inp["L0_tok_W"].T), "pos": tiled(np.tile(pos, (IMGS, 1))),
        "bias": tiled(np.tile(bias, (IMGS, 1))), "wqkvo": wqkvo, "gateT": rows(inp["L0_ffn_gate_w"].T),
        "gbias": np.broadcast_to(inp["L0_ffn_gate_bias"], (P, TILES, E)), "w13": w13, "w2": w2.transpose(2, 0, 1),
        "ident": np.eye(P, dtype=np.float32), 
        "causal": np.repeat(causal[:, None], HG, axis=1).astype(np.float32),
        "hmask": (np.arange(P)[:, None] // HD == np.arange(HG)).astype(np.float32),
        "vmask": (np.arange(2 * N)[:, None] // N == ch // HD % 2).astype(np.float32),
        "below": np.broadcast_to(np.tri(E, k=-1, dtype=np.float32), (P, E, E)),
        "sel": sel.reshape(96, E, P).astype(np.float32),
    }


def kernel(**inputs):
    import concourse.bacc as _bacc
    from concourse.bass_utils import run_bass_kernel_spmd as _run

    nc = _bacc.Bacc("TRN2", target_bir_lowering=False, num_devices=1)
    laid = _lay_out({k: np.asarray(v) for k, v in inputs.items()})
    arrays, args = {}, []
    for name, a in laid.items():
        a = np.ascontiguousarray(a)
        arrays[f"in_{name}_dram"] = a
        args.append(nc.dram_tensor(f"in_{name}_dram", a.shape, mybir.dt.from_np(a.dtype), kind="ExternalInput").ap())
    args.append(nc.dram_tensor("out_dram", (P, 2, B * N), F32, kind="ExternalOutput").ap())
    build(nc, *args)
    r = _run(nc, [arrays], core_ids=[0])
    got = r.results[0]["out_dram"]
    return np.ascontiguousarray(got.transpose(2, 1, 0)).reshape(B, N, D)
```

```python
from contextlib import ExitStack

import numpy as np

import concourse.bass as bass
from concourse import mybir

ALU = mybir.AluOpType
ACT = mybir.ActivationFunctionType
AX = mybir.AxisListType
F32 = mybir.dt.float32
F32R = mybir.dt.float32r
BF16 = mybir.dt.bfloat16

P = 128
B, N, D = 64, 37, 256
HEADS, HD = 16, 16
PC = 6
E, TOPK = 16, 4
GROUPS, TOPG = 4, 2
ITERS = 8
IMGS = B // ITERS
TOK = IMGS * N
TILES = -(-TOK // P)
ROWS = [min(P, TOK - P * t) for t in range(TILES)]
PAIRS = IMGS // 2
HG = 8
NE = E + 1
EPS = 1e-5
NEG = -1e30
SPAN = 64 + N


FILL = {"next": 1, "norm1": 1, "turn1": 1, "v": 1, "att0a": 1, "att1a": 1, "att1b": 1, "att2a": 1, "att2b": 1,
        "att3a": 1, "att3b": 1, "att4a": 1, "att4b": 1, "wo": 1, "norm2": 1, "turn2": 1,
        "route0": 1, "route1": 1, "route2": 1}
assert sum(FILL.values()) == NE + 2


def build(nc, xT, wpT, pos, bias, wqkvo, gateT, gbias, wexp, ident, causal, hmask, vmask, below, out, comb_dram):
    with ExitStack() as ctx:
        def sb(name, shape, dt=F32):
            return ctx.enter_context(nc.sbuf_tensor(name, shape, dt))

        wp_s = sb("wp_s", [P, PC, D])
        tab = sb("tab", [P, TILES, D])
        w_s = sb("w_s", [P, 4, 2, D])
        gate_s = sb("gate_s", [P, 2, E])
        gb_s = sb("gb_s", [P, TILES, E])
        wexp_h = sb("wexp_h", [P, NE, 6, P], F32R)
        wexp_l = sb("wexp_l", [P, NE, 6, P], F32R)
        id_s = sb("id_s", [P, P])
        idb_s = sb("idb_s", [P, N], BF16)
        causal_s = sb("causal_s", [P, HG, N], BF16)
        hmask_s = sb("hmask_s", [P, HG])
        vmask_s = sb("vmask_s", [2 * N, 2])
        below_s = sb("below_s", [P, E, E])
        half_s = sb("half_s", [P, 1])
        eps_s = sb("eps_s", [P, 1])
        shared_s = sb("shared_s", [P, 1])
        x_s = sb("x_s", [P, PC, TOK])
        h_nat = sb("h_nat", [P, TILES, D])
        xn = sb("xn", [P, TILES, D])
        h2 = sb("h2", [P, TILES, D])
        hnT = h2[:].rearrange("p t d -> p (t d)")[:, 0:2 * TOK].rearrange("p (c t) -> p c t", c=2)
        tT = sb("tT", [P, 4, TOK])
        v_sb = tT[:].rearrange("p a t -> p (a t)")[0:2 * N, 0:PAIRS * D].rearrange("p (m d) -> p m d", d=D)
        st = sb("st", [P, 2, TILES, 6])
        mv = sb("mv", [P, 2, TILES, 2])
        ve = sb("ve", [P, 2, TILES])
        rstd = sb("rstd", [P, 2, TILES])
        qT = sb("qT", [P, 2, IMGS, N])
        kT = sb("kT", [P, 2, IMGS, N])
        oT = qT[:].rearrange("p g m t -> p g (m t)")
        work = sb("work", [P, 4 * HG * N + 2 * HEADS * N])
        bdk = work[:, 0:4 * HG * N].rearrange("p (g m n) -> p g m n", g=2, m=2)
        ex = work[:, 4 * HG * N:].rearrange("p (b h k) -> p b h k", b=2, h=HEADS)
        ecmp = work[:, 0:2 * TILES * E * E].rearrange("p (s t e f) -> p s t e f", s=2, t=TILES, e=E)
        causal_f = work[:, 0:HG * N].rearrange("p (h k) -> p h k", h=HG)
        tmp = sb("tmp", [P, 12 * P])
        raw = tmp[:].rearrange("p (b c q) -> p b c q", b=2, c=6)
        th, s1, us, gs = (tmp[:, TOK * n:TOK * n + TOK] for n in range(4))
        bdv = sb("bdv", [2 * N, IMGS, D])
        nmax = sb("nmax", [P, 2, HEADS])
        rsum = sb("rsum", [P, 2, HEADS])
        rinv = sb("rinv", [P, 2, HEADS])
        ptT = sb("ptT", [2 * N, 8, 2, N])
        lg = sb("lg", [P, TILES, E])
        lg1 = sb("lg1", [P, TILES, E])
        sc = sb("sc", [P, TILES, E])
        biased = sb("biased", [P, TILES, E])
        gmax = sb("gmax", [P, TILES, GROUPS])
        gcmp = sb("gcmp", [P, 2, TILES, GROUPS, GROUPS])
        grank = sb("grank", [P, TILES, GROUPS])
        keep = sb("keep", [P, TILES, GROUPS])
        kneg = sb("kneg", [P, TILES, GROUPS])
        sm = sb("sm", [P, TILES, E])
        rank = sb("rank", [P, TILES, E])
        comb = sb("comb", [P, TILES, E])
        combT = sb("combT", [E, TOK])
        x_h = sb("x_h", [P, 2, 2, TOK], F32R)
        x_l = sb("x_l", [P, 2, 2, TOK], F32R)
        h2T = sb("h2T", [P, 2, 2, TOK])
        cb = sb("cb", [P, 2, 2, TOK])
        g_h = sb("g_h", [P, 2, TOK], F32R)
        g_l = sb("g_l", [P, 2, TOK], F32R)
        yo = sb("yo", [P, 2, TOK])

        front = [ctx.enter_context(nc.psum_tensor(f"front{b}", [P, 512], F32)) for b in range(4)]
        ps_h1, ps_h3, ps_y0, ps_y1 = (ctx.enter_context(nc.psum_tensor(n, [P, 512], F32))
                                      for n in ("ps_h1", "ps_h3", "ps_y0", "ps_y1"))

        names = """x_in w_in raw_in0 raw_in1 raw_h raw_l tab_sum init
        banks_zero wp_in table_in v_ok v_in patched h_ok h_stat h_agg h_var h_rstd xn_ok xT_ps hnT_ok qk_ps qk_ok v_ps bdv_ok
        bdk0 bdk1 s_ps s_max s_sub s_exp s_sum s_inv s_norm pt_ps pt_ok o_ps o_ok
        wo_ps h2_ok h2_stat h2_agg h2_var h2_rstd x2_ok t2_ps t2_ok xh_ok xl_ok h2T_ok lg_ps lg_exp
        route_step comb_ok ct_ps ct_ok cb_stored cb_in0 cb_in1
        up_ps th_ok s1_ok u_ok g_ok gh_ok gl_ok y_ps yo_ok stored""".split()
        S = {n: ctx.enter_context(nc.semaphore(n)) for n in names}
        block = ctx.enter_context(nc.Block())
        TABLE_LOADS = 3
        CONST_LOADS = 7
        INITS = 6
        ROUTE_STEPS = 18
        PATCH_BANKS = (2, 3, 0)

        def tile(t):
            return slice(P * t, P * t + ROWS[t])

        def parity(buf, i):
            return buf[:, bass.ds(i % 2, 1)].rearrange("p b c t -> p (b c) t")

        def passes(slot):
            before = 0
            for name, n in FILL.items():
                if name == slot:
                    return range(before - 1, before - 1 + n)
                before += n
            return range(0)

        @block.sync
        def _(sp):
            sp.dma_start(wp_s[:], wpT).then_inc(S["wp_in"], 16)
            for dst, src in ((tab[:], pos), (h2[:], bias), (id_s[:], ident)):
                sp.dma_start(dst, src).then_inc(S["table_in"], 16)
            for dst, src in ((w_s[:], wqkvo), (causal_f, causal), (hmask_s[:], hmask), (vmask_s[:], vmask), (gate_s[:], gateT),
                             (gb_s[:], gbias), (below_s[:], below)):
                sp.dma_start(dst, src).then_inc(S["w_in"], 16)
            def load_experts(es):
                for e in es:
                    if e >= 2:
                        sp.wait_ge(S["raw_l"], e - 1)
                    sp.dma_start(raw[:, e % 2], wexp[:, e]).then_inc(S[f"raw_in{e % 2}"], 16)

            def values(i, more):
                sp.wait_ge(S["v_ok"], (i + 1) * PAIRS)
                for r in range(2):
                    for im in range(2):
                        sp.dma_start(bdv[N * r:N * r + N].rearrange("t (p m) d -> t p m d", m=2)[:, :, im],
                                     v_sb[N * im:N * im + N]).then_inc(S["v_in"], 16)
                if more:
                    sp.wait_ge(S["patched"], (i + 1) * TILES)
                    sp.dma_start(x_s[:], xT[bass.ds(i + 1, 1)].rearrange("i p c t -> p (i c) t")) \
                        .then_inc(S["x_in"], 16)

            def weights_rows(i, first):
                sp.wait_ge(S["ct_ok"], i + 1)
                sp.dma_start(comb_dram[bass.ds(i, 1)].rearrange("i e t -> (i e) t"), combT[:]) \
                    .then_inc(S["cb_stored"], 16)
                if not first:
                    sp.wait_ge(S["yo_ok"], i)
                    sp.dma_start(out[:, :, bass.ds((i - 1) * TOK, TOK)], yo[:]).then_inc(S["stored"], 16)
                sp.wait_ge(S["cb_stored"], (i + 1) * 16)

            def spread(i, q, first):
                if q >= 2:
                    sp.wait_ge(S["g_ok"], i * NE + 2 * q - 1)
                elif not first:
                    sp.wait_ge(S["g_ok"], (i - 1) * NE + NE - 2 + 2 * q)
                src = comb_dram[bass.ds(i, 1), 2 * q:2 * q + 2].rearrange("i e t -> i (e t)")
                sp.dma_start(cb[:, q % 2].rearrange("p e t -> p (e t)"), src.to_broadcast([P, 2 * TOK])) \
                    .then_inc(S[f"cb_in{q % 2}"], 16)

            def iteration(i, first, more):
                weights_rows(i, first)
                for q in range(2):
                    spread(i, q, first)
                values(i + 1, more)
                for q in range(2, E // 2):
                    spread(i, q, first)

            sp.sem_inc(S["stored"], 16)
            load_experts(range(2))
            values(0, True)
            load_experts(range(2, NE))
            iteration(0, True, True)
            with sp.Fori(1, ITERS - 2) as i:
                iteration(i, False, True)
            iteration(ITERS - 2, False, False)
            weights_rows(ITERS - 1, False)
            for q in range(E // 2):
                spread(ITERS - 1, q, False)
            for slot in range(2):
                sp.wait_ge(S[f"cb_in{slot}"], 16 * ITERS * E // 4)
            sp.wait_ge(S["yo_ok"], ITERS)
            sp.dma_start(out[:, :, (ITERS - 1) * TOK:ITERS * TOK], yo[:]).then_inc(S["stored"], 16)
            sp.wait_ge(S["stored"], 16 * (ITERS + 1))

        @block.gpsimd
        def _(pool):
            pool.memset(half_s[:], -0.5).then_inc(S["init"], 1)
            pool.memset(eps_s[:], EPS).then_inc(S["init"], 1)
            pool.memset(shared_s[:], 0.5).then_inc(S["init"], 1)
            pool.wait_ge(S["init"], INITS)
            pool.wait_ge(S["w_in"], 16 * CONST_LOADS)

            def weigh(j, k):
                pool.wait_ge(S["u_ok"], j * NE + k + 1)
                if k >= 1:
                    q = (k - 1) // 2
                    pool.wait_ge(S[f"cb_in{q % 2}"], 16 * (j * (E // 4) + q // 2 + 1))
                if k >= 1:
                    pool.wait_ge(S["gl_ok"], j * NE + k)
                weights = cb[:, (k - 1) // 2 % 2, (k - 1) % 2] if k else shared_s[:].to_broadcast([P, TOK])
                pool.tensor_tensor(gs, us, weights, ALU.mult).then_inc(S["g_ok"], 1)

            def experts(j, slot):
                if j is not None:
                    for k in passes(slot):
                        if k + 1 < NE:
                            weigh(j, k + 1)

            def rstds(i, which, agg, var, done):
                for t in range(TILES):
                    r = ROWS[t]
                    pool.wait_ge(S[agg], i * TILES + t + 1)
                    pool.tensor_tensor(ve[0:r, which, t:t + 1], mv[0:r, which, t, 1:2], eps_s[0:r],
                                       ALU.add).then_inc(S[var], 1)
                    pool.wait_ge(S[var], i * TILES + t + 1)
                    pool.tensor_tensor(rstd[0:r, which, t:t + 1], ve[0:r, which, t:t + 1], half_s[0:r],
                                       ALU.pow).then_inc(S[done], 1)

            def split_weights(es):
                for e in es:
                    pool.wait_ge(S["raw_h"], e + 1)
                    pool.tensor_tensor(wexp_l[:, e], raw[:, e % 2], wexp_h[:, e].bitcast(F32),
                                       ALU.subtract).then_inc(S["raw_l"], 1)

            def iteration(i, j):
                rstds(i, 0, "h_agg", "h_var", "h_rstd")
                for slot in ("norm1", "turn1"):
                    experts(j, slot)

                def heads_apart(p):
                    if p == 0:
                        pool.wait_ge(S["qk_ok"], i * 4 + 4)
                    else:
                        pool.wait_ge(S["s_ps"], i * PAIRS + p)
                    pool.tensor_tensor(
                        bdk[:, 1].rearrange("p m (h k) -> p m h k", h=HG),
                        kT[:, 1, 2 * p:2 * p + 2, None, :].to_broadcast([P, 2, HG, N]),
                        hmask_s[:, None, :, None].to_broadcast([P, 2, HG, N]),
                        ALU.mult).then_inc(S["bdk1"], 1)

                heads_apart(0)
                experts(j, "v")
                for p in range(PAIRS + 1):
                    experts(j, f"att{p}a")
                    if p + 1 < PAIRS:
                        heads_apart(p + 1)
                    if p < PAIRS:
                        pool.wait_ge(S["s_inv"], i * PAIRS + p + 1)
                        pool.tensor_tensor(ex[0:SPAN, p % 2], ex[0:SPAN, p % 2],
                                           rinv[0:SPAN, p % 2, :, None].to_broadcast([SPAN, HEADS, N]),
                                           ALU.mult).then_inc(S["s_norm"], 1)
                    if j is None:
                        split_weights(range(4 * p, min(4 * p + 4, NE)))
                    experts(j, f"att{p}b")
                experts(j, "wo")
                rstds(i, 1, "h2_agg", "h2_var", "h2_rstd")
                for slot in ("norm2", "turn2", "route0", "route1", "route2"):
                    experts(j, slot)
                experts(i, "next")

            iteration(0, None)
            with pool.Fori(1, ITERS) as i:
                iteration(i, i - 1)
            for slot in list(FILL)[1:]:
                experts(ITERS - 1, slot)

        @block.scalar
        def _(act):
            act.dma_start(x_s[:], xT[0]).then_inc(S["x_in"], 16)

            def experts(j, slot):
                if j is not None:
                    for k in passes(slot):
                        if 0 <= k < NE:
                            act.wait_ge(S["g_ok"], j * NE + k + 1)
                            if k >= 2:
                                act.wait_ge(S["y_ps"], j * NE + k - 1)
                            act.activation(g_h[:, k % 2], gs, ACT.Copy).then_inc(S["gh_ok"], 1)
                        if k + 1 < NE:
                            act.wait_ge(S["up_ps"], j * NE + k + 2)
                            if k >= 0:
                                act.wait_ge(S["s1_ok"], j * NE + k + 1)
                            act.activation(th, ps_h1[:, 0:TOK], ACT.Tanh, scale=0.5).then_inc(S["th_ok"], 1)

            def split_weights(es):
                for e in es:
                    act.wait_ge(S[f"raw_in{e % 2}"], 16 * (e // 2 + 1))
                    act.activation(wexp_h[:, e], raw[:, e % 2], ACT.Copy).then_inc(S["raw_h"], 1)

            def iteration(i, j):
                experts(j, "norm1")
                for t in range(TILES):
                    act.wait_ge(S["xT_ps"], i * TILES + t + 1)
                    act.activation(hnT[:, :, tile(t)],
                                   front[2 + t % 2][:, 0:2 * P].rearrange("p (c t) -> p c t", c=2)[:, :, 0:ROWS[t]],
                                   ACT.Copy).then_inc(S["hnT_ok"], 1)
                experts(j, "turn1")
                for n in range(4):
                    g, is_k = divmod(n, 2)
                    act.wait_ge(S["qk_ps"], i * 4 + n + 1)
                    act.activation((kT if is_k else qT)[:, g], front[n][:, 0:TOK].rearrange("p (m t) -> p m t", t=N),
                                   ACT.Copy, scale=1.0 if is_k else HD ** -0.5).then_inc(S["qk_ok"], 1)
                for p in range(PAIRS):
                    act.wait_ge(S["v_ps"], i * PAIRS + p + 1)
                    act.activation(v_sb[:, p], front[p][0:2 * N, 0:D], ACT.Copy).then_inc(S["v_ok"], 1)
                experts(j, "v")
                for p in range(PAIRS + 1):
                    experts(j, f"att{p}a")
                    if p < PAIRS:
                        act.wait_ge(S["s_sub"], i * PAIRS + p + 1)
                        act.activation(ex[0:SPAN, p % 2], ex[0:SPAN, p % 2], ACT.Exp).then_inc(S["s_exp"], 1)
                    if p >= 1:
                        q = p - 1
                        for hf in range(2):
                            act.wait_ge(S["pt_ps"], (i * PAIRS + q) * 2 + hf + 1)
                            act.activation(
                                ptT[:, 4 * hf:4 * hf + 4],
                                front[2 + hf][0:2 * N, :].rearrange("p (c m t) -> p c m t", c=4, m=2)[:, :, :, 0:N],
                                ACT.Copy).then_inc(S["pt_ok"], 1)
                    if p < PAIRS:
                        act.wait_ge(S["v_in"], (i + 1) * 64)
                        for odd in range(2):
                            vals = bdv[:, 2 * p:2 * p + 2].rearrange("t m (g o d) -> t (m g) o d", o=2, d=HD)[:, :, odd]
                            act.activation(vals, vals, ACT.Copy, scale=vmask_s[:, odd:odd + 1]).then_inc(S["bdv_ok"], 1)
                    if j is None:
                        split_weights(range(4 * p, min(4 * p + 4, NE)))
                    experts(j, f"att{p}b")
                experts(j, "wo")
                experts(j, "norm2")
                for t in range(TILES):
                    act.wait_ge(S["t2_ps"], i * TILES + t + 1)
                    act.activation(tT[:, :, tile(t)],
                                   front[2 + t % 2][:].rearrange("p (c t) -> p c t", c=4)[:, :, 0:ROWS[t]],
                                   ACT.Copy).then_inc(S["t2_ok"], 1)
                act.wait_ge(S["w_in"], 16 * CONST_LOADS)
                act.wait_ge(S["t2_ok"], (i + 1) * TILES)
                act.activation(parity(x_h, i), tT[:, 2:4], ACT.Copy).then_inc(S["xh_ok"], 1)
                experts(j, "turn2")
                act.wait_ge(S["lg_ps"], i + 1)
                act.activation(lg[:], front[0][:, 0:TILES * E].rearrange("p (t e) -> p t e", e=E), ACT.Exp,
                               scale=-1.0).then_inc(S["lg_exp"], 1)
                for slot in ("route0", "route1", "route2"):
                    experts(j, slot)
                experts(i, "next")
                act.wait_ge(S["ct_ps"], i + 1)
                act.activation(combT[:], front[1][0:E, 0:TOK], ACT.Copy).then_inc(S["ct_ok"], 1)

            iteration(0, None)
            with act.Fori(1, ITERS) as i:
                iteration(i, i - 1)
            for slot in list(FILL)[1:]:
                experts(ITERS - 1, slot)

        @block.vector
        def _(dve):
            for b in front:
                dve.memset(b[:], 0.0).then_inc(S["banks_zero"], 1)
            dve.memset(xn[:], 0.0).then_inc(S["init"], 1)
            dve.wait_ge(S["table_in"], 16 * TABLE_LOADS)
            dve.tensor_tensor(tab[:], tab[:], h2[:], ALU.add).then_inc(S["tab_sum"], 1)
            dve.wait_ge(S["w_in"], 16 * CONST_LOADS)
            dve.tensor_copy(idb_s[:], id_s[:, 0:N]).then_inc(S["init"], 1)
            dve.tensor_copy(causal_s[:], causal_f).then_inc(S["init"], 1)
            dve.wait_ge(S["tab_sum"], 1)

            def experts(j, slot):
                if j is None:
                    return
                for k in passes(slot):
                    if 0 <= k < NE:
                        dve.wait_ge(S["gh_ok"], j * NE + k + 1)
                        if k >= 2:
                            dve.wait_ge(S["y_ps"], j * NE + k - 1)
                        dve.tensor_tensor(g_l[:, k % 2], gs, g_h[:, k % 2].bitcast(F32),
                                          ALU.subtract).then_inc(S["gl_ok"], 1)
                    if k + 1 < NE:
                        dve.wait_ge(S["th_ok"], j * NE + k + 2)
                        dve.scalar_tensor_tensor(s1, th, 1.0, ps_h1[:, 0:TOK], ALU.add,
                                                 ALU.mult).then_inc(S["s1_ok"], 1)
                        dve.wait_ge(S["s1_ok"], j * NE + k + 2)
                        if k >= 0:
                            dve.wait_ge(S["g_ok"], j * NE + k + 1)
                        dve.tensor_tensor(us, s1, ps_h3[:, 0:TOK],
                                          ALU.mult).then_inc(S["u_ok"], 1)
                if slot == "route2":
                    dve.wait_ge(S["y_ps"], (j + 1) * NE)
                    dve.wait_ge(S["stored"], 16 * (j + 1))
                    res = parity(h2T, j)
                    dve.tensor_tensor(yo[:, 0], ps_y0[:, 0:TOK], res[:, 0], ALU.add)
                    dve.tensor_tensor(yo[:, 1], ps_y1[:, 0:TOK], res[:, 1], ALU.add).then_inc(S["yo_ok"], 1)

            def iteration(i, j):
                def layernorm(which, banks, ps, other, res, pre, done):
                    for t in range(TILES):
                        r = ROWS[t]
                        dve.wait_ge(S[ps], i * TILES + t + 1)
                        dve.tensor_tensor(res[0:r, t], front[banks[t]][0:r, 0:D], other[0:r, t],
                                          ALU.add).then_inc(S[pre + "_ok"], 1)
                        dve.wait_ge(S[pre + "_ok"], i * TILES + t + 1)
                        dve.bn_stats(st[0:r, which, t], res[0:r, t]).then_inc(S[pre + "_stat"], 1)
                        dve.wait_ge(S["w_in"], 16 * CONST_LOADS)
                        dve.wait_ge(S[pre + "_stat"], i * TILES + t + 1)
                        dve.bn_aggr(mv[0:r, which, t], st[0:r, which, t]).then_inc(S[pre + "_agg"], 1)
                    for t in range(TILES):
                        r = ROWS[t]
                        dve.wait_ge(S[pre + "_agg"], i * TILES + t + 1)
                        dve.wait_ge(S[pre + "_rstd"], i * TILES + t + 1)
                        dve.tensor_scalar(xn[0:r, t], res[0:r, t], mv[0:r, which, t, 0:1],
                                          rstd[0:r, which, t:t + 1], ALU.subtract, ALU.mult).then_inc(S[done], 1)

                layernorm(0, PATCH_BANKS, "patched", tab, h_nat, "h", "xn_ok")
                experts(j, "norm1")
                experts(j, "turn1")
                def heads_apart(p):
                    if p == 0:
                        dve.wait_ge(S["qk_ok"], i * 4 + 4)
                    if p >= 1:
                        dve.wait_ge(S["s_ps"], i * PAIRS + p)
                    dve.tensor_tensor(
                        bdk[:, 0].rearrange("p m (h k) -> p m h k", h=HG),
                        kT[:, 0, 2 * p:2 * p + 2, None, :].to_broadcast([P, 2, HG, N]),
                        hmask_s[:, None, :, None].to_broadcast([P, 2, HG, N]),
                        ALU.mult).then_inc(S["bdk0"], 1)

                heads_apart(0)
                experts(j, "v")
                for p in range(PAIRS + 1):
                    if p < PAIRS:
                        dve.wait_ge(S["s_ps"], i * PAIRS + p + 1)
                        for g in range(2):
                            a = dve.tensor_reduce(nmax[0:SPAN, p % 2, HG * g:HG * g + HG],
                                                  front[g][0:SPAN, 0:HG * N].rearrange("p (h k) -> p h k", h=HG),
                                                  AX.X, ALU.max, negate=True)
                        a.then_inc(S["s_max"], 1)
                        dve.wait_ge(S["s_max"], i * PAIRS + p + 1)
                        if p >= 2:
                            dve.wait_ge(S["pt_ps"], (i * PAIRS + p - 1) * 2)
                        for g in range(2):
                            a = dve.tensor_tensor(
                                ex[0:SPAN, p % 2, HG * g:HG * g + HG],
                                front[g][0:SPAN, 0:HG * N].rearrange("p (h k) -> p h k", h=HG),
                                nmax[0:SPAN, p % 2, HG * g:HG * g + HG, None].to_broadcast([SPAN, HG, N]), ALU.add)
                        a.then_inc(S["s_sub"], 1)
                    experts(j, f"att{p}a")
                    if p + 1 < PAIRS:
                        heads_apart(p + 1)
                    if p < PAIRS:
                        dve.wait_ge(S["s_exp"], i * PAIRS + p + 1)
                        dve.tensor_reduce(rsum[0:SPAN, p % 2], ex[0:SPAN, p % 2], AX.X,
                                          ALU.add).then_inc(S["s_sum"], 1)
                        dve.wait_ge(S["s_sum"], i * PAIRS + p + 1)
                        dve.reciprocal(rinv[0:SPAN, p % 2], rsum[0:SPAN, p % 2]).then_inc(S["s_inv"], 1)
                    experts(j, f"att{p}b")
                    if p >= 1:
                        q = p - 1
                        dve.wait_ge(S["o_ps"], i * PAIRS + q + 1)
                        dve.tensor_copy(oT[:, :, 2 * N * q:2 * N * (q + 1)],
                                        front[2][:, 0:4 * N].rearrange("p (g t) -> p g t", g=2)) \
                            .then_inc(S["o_ok"], 1)
                experts(j, "wo")
                layernorm(1, (0, 1, 0), "wo_ps", h_nat, h2, "h2", "x2_ok")
                experts(j, "norm2")
                dve.wait_ge(S["w_in"], 16 * CONST_LOADS)
                dve.wait_ge(S["t2_ok"], (i + 1) * TILES)
                dve.tensor_copy(parity(h2T, i), tT[:, 0:2]).then_inc(S["h2T_ok"], 1)
                dve.wait_ge(S["xh_ok"], i + 1)
                dve.tensor_tensor(parity(x_l, i), tT[:, 2:4], parity(x_h, i).bitcast(F32),
                                  ALU.subtract).then_inc(S["xl_ok"], 1)
                experts(j, "turn2")

                r = i * ROUTE_STEPS
                dve.wait_ge(S["lg_exp"], i + 1)
                dve.tensor_scalar(lg1[:], lg[:], 1.0, None, ALU.add).then_inc(S["route_step"], 1)
                dve.wait_ge(S["route_step"], r + 1)
                dve.reciprocal(sc[:], lg1[:]).then_inc(S["route_step"], 1)
                dve.wait_ge(S["route_step"], r + 2)
                dve.tensor_tensor(biased[:], sc[:], gb_s[:], ALU.add).then_inc(S["route_step"], 1)
                dve.wait_ge(S["route_step"], r + 3)
                by_group = biased[:].rearrange("p t (g k) -> p (t g) k", g=GROUPS)
                dve.tensor_reduce(gmax[:].rearrange("p t g -> p (t g)"), by_group, AX.X, ALU.max).then_inc(S["route_step"], 1)
                dve.wait_ge(S["route_step"], r + 4)
                mine = gmax[:, :, :, None].to_broadcast([P, TILES, GROUPS, GROUPS])
                other = gmax[:, :, None, :].to_broadcast([P, TILES, GROUPS, GROUPS])
                lower = below_s[:, None, 0:GROUPS, 0:GROUPS].to_broadcast([P, TILES, GROUPS, GROUPS])
                dve.tensor_tensor(gcmp[:, 0], other, mine, ALU.is_gt)
                dve.tensor_tensor(gcmp[:, 1], other, mine, ALU.is_equal).then_inc(S["route_step"], 1)
                dve.wait_ge(S["route_step"], r + 5)
                dve.tensor_tensor(gcmp[:, 1], gcmp[:, 1], lower, ALU.mult).then_inc(S["route_step"], 1)
                dve.wait_ge(S["route_step"], r + 6)
                dve.tensor_tensor(gcmp[:, 0], gcmp[:, 0], gcmp[:, 1], ALU.add).then_inc(S["route_step"], 1)
                dve.wait_ge(S["route_step"], r + 7)
                dve.tensor_reduce(grank[:], gcmp[:, 0], AX.X, ALU.add).then_inc(S["route_step"], 1)
                dve.wait_ge(S["route_step"], r + 8)
                experts(j, "route0")
                dve.tensor_scalar(keep[:], grank[:], float(TOPG), None, ALU.is_lt).then_inc(S["route_step"], 1)
                dve.wait_ge(S["route_step"], r + 9)
                dve.tensor_scalar(kneg[:], keep[:], -1.0, -NEG, ALU.add, ALU.mult).then_inc(S["route_step"], 1)
                dve.wait_ge(S["route_step"], r + 10)
                masked = sm[:].rearrange("p t (g k) -> p (t g) k", g=GROUPS)
                shape = [P, TILES * GROUPS, E // GROUPS]
                dve.tensor_tensor(masked, by_group,
                                  keep[:].rearrange("p t g -> p (t g)")[:, :, None].to_broadcast(shape), ALU.mult).then_inc(S["route_step"], 1)
                dve.wait_ge(S["route_step"], r + 11)
                dve.tensor_tensor(masked, masked,
                                  kneg[:].rearrange("p t g -> p (t g)")[:, :, None].to_broadcast(shape), ALU.add).then_inc(S["route_step"], 1)
                dve.wait_ge(S["route_step"], r + 12)
                experts(j, "route1")
                mine = sm[:, :, :, None].to_broadcast([P, TILES, E, E])
                other = sm[:, :, None, :].to_broadcast([P, TILES, E, E])
                lower = below_s[:, None, 0:E, 0:E].to_broadcast([P, TILES, E, E])
                dve.tensor_tensor(ecmp[:, 0], other, mine, ALU.is_gt)
                dve.tensor_tensor(ecmp[:, 1], other, mine, ALU.is_equal).then_inc(S["route_step"], 1)
                dve.wait_ge(S["route_step"], r + 13)
                dve.tensor_tensor(ecmp[:, 1], ecmp[:, 1], lower, ALU.mult).then_inc(S["route_step"], 1)
                dve.wait_ge(S["route_step"], r + 14)
                dve.tensor_tensor(ecmp[:, 0], ecmp[:, 0], ecmp[:, 1], ALU.add).then_inc(S["route_step"], 1)
                dve.wait_ge(S["route_step"], r + 15)
                dve.tensor_reduce(rank[:], ecmp[:, 0], AX.X, ALU.add).then_inc(S["route_step"], 1)
                dve.wait_ge(S["route_step"], r + 16)
                dve.tensor_scalar(rank[:], rank[:], float(TOPK), 0.5, ALU.is_lt, ALU.mult).then_inc(S["route_step"], 1)
                dve.wait_ge(S["route_step"], r + 17)
                dve.tensor_tensor(comb[:], rank[:], sc[:], ALU.mult).then_inc(S["route_step"], 1)
                experts(j, "route2")
                experts(i, "next")

            iteration(0, None)
            with dve.Fori(1, ITERS) as i:
                iteration(i, i - 1)
            for slot in list(FILL)[1:]:
                experts(ITERS - 1, slot)

        @block.tensor
        def _(pe):
            def patch(t):
                for c in range(PC):
                    m = pe.matmul(front[PATCH_BANKS[t]][0:ROWS[t], 0:D], x_s[:, c, tile(t)], wp_s[:, c],
                                  start=(c == 0), stop=(c == PC - 1))
                m.then_inc(S["patched"], 1)

            pe.wait_ge(S["banks_zero"], len(front))
            pe.wait_ge(S["x_in"], 16)
            pe.wait_ge(S["wp_in"], 16)
            for t in range(TILES):
                patch(t)
            pe.wait_ge(S["w_in"], 16 * CONST_LOADS)
            pe.wait_ge(S["init"], INITS)

            def split_product(o, stat_h, stat_l, mov_h, mov_l, first, last):
                pe.matmul(o, stat_h, mov_h, start=first, stop=False)
                pe.matmul(o, stat_h, mov_l, start=False, stop=False)
                return pe.matmul(o, stat_l, mov_h, start=False, stop=last)

            def up(j, k):
                for w, o in ((0, ps_h1), (1, ps_h3)):
                    if k >= 1 and w == 0:
                        pe.wait_ge(S["s1_ok"], j * NE + k)
                    if k >= 1 and w == 1:
                        pe.wait_ge(S["u_ok"], j * NE + k)
                    for d in range(2):
                        c = 2 * w + d
                        m = split_product(o[:, 0:TOK], wexp_h[:, k, c], wexp_l[:, k, c],
                                          parity(x_h, j)[:, d], parity(x_l, j)[:, d], d == 0, d == 1)
                m.then_inc(S["up_ps"], 1)

            def down(j, k):
                pe.wait_ge(S["gl_ok"], j * NE + k + 1)
                for d, o in ((0, ps_y0), (1, ps_y1)):
                    m = split_product(o[:, 0:TOK], wexp_h[:, k, 4 + d], wexp_l[:, k, 4 + d],
                                      g_h[:, k % 2], g_l[:, k % 2], k == 0, k == NE - 1)
                m.then_inc(S["y_ps"], 1)

            def experts(j, slot):
                if j is None:
                    return
                for k in passes(slot):
                    if k == -1:
                        pe.wait_ge(S["xl_ok"], j + 1)
                    if k + 1 < NE:
                        up(j, k + 1)
                    if 1 <= k <= NE:
                        down(j, k - 1)

            def iteration(i, j, more):
                experts(j, "norm1")
                for t in range(TILES):
                    pe.wait_ge(S["xn_ok"], i * TILES + t + 1)
                    if t >= 2:
                        pe.wait_ge(S["hnT_ok"], i * TILES + t - 1)
                    for c in range(2):
                        m = pe.transpose(front[2 + t % 2][:, P * c:P * c + P], xn[:, t, P * c:P * c + P], id_s[:])
                    m.then_inc(S["xT_ps"], 1)
                experts(j, "turn1")
                pe.wait_ge(S["hnT_ok"], (i + 1) * TILES)
                for n in range(4):
                    g, is_k = divmod(n, 2)
                    if n == 1 and j is not None:
                        pe.wait_ge(S["ct_ok"], i)
                    for c in range(2):
                        m = pe.matmul(front[n][:, 0:TOK], w_s[:, is_k, c, P * g:P * g + P], hnT[:, c],
                                      start=(c == 0), stop=(c == 1))
                    m.then_inc(S["qk_ps"], 1)
                for p in range(PAIRS):
                    pe.wait_ge(S["qk_ok"], i * 4 + p + 1)
                    for c in range(2):
                        m = pe.matmul(front[p][0:2 * N, 0:D], hnT[:, c, 2 * N * p:2 * N * (p + 1)], w_s[:, 2, c],
                                      start=(c == 0), stop=(c == 1))
                    m.then_inc(S["v_ps"], 1)
                experts(j, "v")
                for p in range(PAIRS + 1):
                    if p < PAIRS:
                        pe.wait_ge(S["bdk0"], i * PAIRS + p + 1)
                        pe.wait_ge(S["bdk1"], i * PAIRS + p + 1)
                        if p == 0:
                            pe.wait_ge(S["v_ok"], (i + 1) * PAIRS)
                        else:
                            pe.wait_ge(S["s_sub"], i * PAIRS + p)
                        for g in range(2):
                            for im in range(2):
                                o = front[g][64 * im:64 * im + N, 0:HG * N]
                                pe.matmul(o, idb_s[:], causal_s[:].rearrange("k h q -> k (h q)"),
                                          start=True, stop=False)
                                m = pe.matmul(o, qT[:, g, 2 * p + im], bdk[:, g, im], start=False, stop=True)
                        m.then_inc(S["s_ps"], 1)
                    experts(j, f"att{p}a")
                    if p >= 1:
                        q = p - 1
                        pe.wait_ge(S["s_norm"], i * PAIRS + q + 1)
                        if q >= 1:
                            pe.wait_ge(S["o_ok"], i * PAIRS + q)
                        for hf in range(2):
                            for c in range(4):
                                h = 8 * hf + 2 * c
                                m = pe.transpose(front[2 + hf][0:2 * N, P * c:P * c + SPAN],
                                                 ex[0:SPAN, q % 2, h:h + 2].rearrange("p h k -> p (h k)"),
                                                 id_s[0:SPAN, 0:SPAN])
                            m.then_inc(S["pt_ps"], 1)
                    experts(j, f"att{p}b")
                    if p >= 1:
                        pe.wait_ge(S["bdv_ok"], (i * PAIRS + q + 1) * 2)
                        for hf in range(2):
                            pe.wait_ge(S["pt_ok"], (i * PAIRS + q) * 2 + hf + 1)
                            for im in range(2):
                                for c in range(4):
                                    col = 2 * N * hf + N * im
                                    m = pe.matmul(front[2][32 * c:32 * c + 32, col:col + N],
                                                  bdv[:, 2 * q + im, P * hf + 32 * c:P * hf + 32 * c + 32],
                                                  ptT[:, 4 * hf + c, im], start=True, stop=True)
                        m.then_inc(S["o_ps"], 1)
                experts(j, "wo")
                pe.wait_ge(S["o_ok"], (i + 1) * PAIRS)
                for t in range(TILES):
                    if t >= 2:
                        pe.wait_ge(S["h2_ok"], i * TILES + t - 1)
                    for c in range(2):
                        m = pe.matmul(front[t % 2][0:ROWS[t], 0:D], oT[:, c, tile(t)], w_s[:, 3, c],
                                      start=(c == 0), stop=(c == 1))
                    m.then_inc(S["wo_ps"], 1)
                experts(j, "norm2")
                for t in range(TILES):
                    pe.wait_ge(S["x2_ok"], i * TILES + t + 1)
                    if t >= 2:
                        pe.wait_ge(S["t2_ok"], i * TILES + t - 1)
                    for c in range(4):
                        src = h2 if c < 2 else xn
                        m = pe.transpose(front[2 + t % 2][:, P * c:P * c + P], src[:, t, P * (c % 2):P * (c % 2) + P],
                                         id_s[:])
                    m.then_inc(S["t2_ps"], 1)
                experts(j, "turn2")
                pe.wait_ge(S["t2_ok"], (i + 1) * TILES)
                for t in range(TILES):
                    for c in range(2):
                        m = pe.matmul(front[0][0:ROWS[t], E * t:E * t + E], tT[:, 2 + c, tile(t)], gate_s[:, c],
                                      start=(c == 0), stop=(c == 1))
                m.then_inc(S["lg_ps"], 1)
                if more:
                    pe.wait_ge(S["x_in"], (i + 2) * 16)
                    patch(0)
                experts(j, "route0")
                if more:
                    patch(1)
                experts(j, "route1")
                if more:
                    pe.wait_ge(S["lg_exp"], i + 1)
                    patch(2)
                experts(j, "route2")
                experts(i, "next")
                pe.wait_ge(S["route_step"], (i + 1) * ROUTE_STEPS)
                for t in range(TILES):
                    m = pe.transpose(front[1][0:E, tile(t)], comb[0:ROWS[t], t], id_s[0:ROWS[t], 0:ROWS[t]])
                m.then_inc(S["ct_ps"], 1)

            iteration(0, None, True)
            with pe.Fori(1, ITERS - 1) as i:
                iteration(i, i - 1, True)
            iteration(ITERS - 1, ITERS - 2, False)
            for slot in list(FILL)[1:]:
                experts(ITERS - 1, slot)


def _lay_out(inp):
    def rows(a):
        return np.ascontiguousarray(a.reshape(-1, P, a.shape[-1]).transpose(1, 0, 2))

    def tiled(a):
        full = np.zeros((TILES * P, a.shape[-1]), a.dtype)
        full[:TOK] = a
        return np.ascontiguousarray(full.reshape(TILES, P, -1).transpose(1, 0, 2))

    x = inp["x"]
    G = x.shape[-1] // 16
    patches = x.reshape(B, 3, G, 16, G, 16).transpose(1, 3, 5, 0, 2, 4).reshape(PC * P, B, G * G)
    xT = np.zeros((PC * P, B, N), x.dtype)
    xT[:, :, 1:] = patches
    xT = xT.reshape(PC, P, ITERS, TOK).transpose(2, 1, 0, 3)
    pos = np.concatenate([inp["cls_tok"][0], inp["L0_tok_pos_embd"][0]])
    bias = np.zeros((N, D), x.dtype)
    bias[1:] = inp["L0_tok_b"]
    wqkvo = np.stack([rows(inp["L0_attn_" + n]) for n in ("Wq", "Wk", "Wv", "Wo")], axis=1)
    w1 = np.concatenate([inp["L0_ffn_ws1"][None], inp["L0_ffn_w1"]])
    w3 = np.concatenate([inp["L0_ffn_ws3"][None], inp["L0_ffn_w3"]])
    w2 = np.concatenate([inp["L0_ffn_ws2"][None], inp["L0_ffn_w2"]])
    up = np.stack([w1, w3], axis=1).reshape(NE, 2, P, 2, P).transpose(4, 0, 1, 3, 2).reshape(P, NE, 4, P)
    down = w2.transpose(2, 0, 1).reshape(P, NE, 2, P)
    ch = np.arange(D)
    causal = np.where(np.arange(N)[None, :] > np.arange(P)[:, None], NEG, 0.0)
    causal[N:] = 0.0
    return {
        "xT": xT, "wpT": rows(inp["L0_tok_W"].T), "pos": tiled(np.tile(pos, (IMGS, 1))),
        "bias": tiled(np.tile(bias, (IMGS, 1))), "wqkvo": wqkvo, "gateT": rows(inp["L0_ffn_gate_w"].T),
        "gbias": np.broadcast_to(inp["L0_ffn_gate_bias"], (P, TILES, E)), "wexp": np.concatenate([up, down], axis=2),
        "ident": np.eye(P, dtype=np.float32), 
        "causal": np.repeat(causal[:, None], HG, axis=1).astype(np.float32),
        "hmask": (np.arange(P)[:, None] // HD == np.arange(HG)).astype(np.float32),
        "vmask": (np.arange(2 * N)[:, None] // N == np.arange(2)).astype(np.float32),
        "below": np.broadcast_to(np.tri(E, k=-1, dtype=np.float32), (P, E, E)),
    }


def kernel(**inputs):
    import concourse.bacc as _bacc
    from concourse.bass_utils import run_bass_kernel_spmd as _run

    nc = _bacc.Bacc("TRN2", target_bir_lowering=False, num_devices=1)
    laid = _lay_out({k: np.asarray(v) for k, v in inputs.items()})
    arrays, args = {}, []
    for name, a in laid.items():
        a = np.ascontiguousarray(a)
        arrays[f"in_{name}_dram"] = a
        args.append(nc.dram_tensor(f"in_{name}_dram", a.shape, mybir.dt.from_np(a.dtype), kind="ExternalInput").ap())
    args.append(nc.dram_tensor("out_dram", (P, 2, B * N), F32, kind="ExternalOutput").ap())
    args.append(nc.dram_tensor("token_weights", (ITERS, E, TOK), F32, kind="Internal").ap())
    build(nc, *args)
    r = _run(nc, [arrays], core_ids=[0])
    got = r.results[0]["out_dram"]
    return np.ascontiguousarray(got.transpose(2, 1, 0)).reshape(B, N, D)
```

```python
from contextlib import ExitStack

import numpy as np

import concourse.bass as bass
from concourse import mybir

ALU = mybir.AluOpType
ACT = mybir.ActivationFunctionType
AX = mybir.AxisListType
F32 = mybir.dt.float32
F32R = mybir.dt.float32r
BF16 = mybir.dt.bfloat16

P = 128
B, N, D = 64, 37, 256
HEADS, HD = 16, 16
PC = 6
E, TOPK = 16, 4
GROUPS, TOPG = 4, 2
ITERS = 8
IMGS = B // ITERS
TOK = IMGS * N
TILES = -(-TOK // P)
ROWS = [min(P, TOK - P * t) for t in range(TILES)]
PAIRS = IMGS // 2
HG = 8
NE = E + 1
EPS = 1e-5
NEG = -1e30
SPAN = 64 + N


FILL = {"next": 1, "norm1": 1, "v": 1, "att0a": 1, "att0b": 1, "att1a": 1, "att1b": 1, "att2a": 1, "att2b": 1,
        "att3a": 1, "att3b": 1, "att4a": 1, "att4b": 1, "wo": 1, "norm2": 1, "turn2": 1,
        "route0": 1, "route1": 1, "route2": 1}
assert sum(FILL.values()) == NE + 2
SPLIT = {"turn1": (0, 1, 2), "v": (3,), "att0b": (4,), "att1b": (5, 6), "att2b": (7,), "att3b": (8, 9),
         "att4b": (10,), "norm2": (11,), "turn2": (12, 13), "route0": (14, 15), "route1": (16,)}
assert sum(SPLIT.values(), ()) == tuple(range(NE))


def build(nc, xT, wpT, pos, bias, wqkvo, gateT, gbias, wexp, ident, causal, hmask, vmask, below, out, comb_dram):
    with ExitStack() as ctx:
        def sb(name, shape, dt=F32):
            return ctx.enter_context(nc.sbuf_tensor(name, shape, dt))

        wp_s = sb("wp_s", [P, PC, D])
        tab = sb("tab", [P, TILES, D])
        w_h = sb("w_h", [P, 4, 2, D], F32R)
        w_l = sb("w_l", [P, 4, 2, D], F32R)
        gate_s = sb("gate_s", [P, 2, E])
        gb_s = sb("gb_s", [P, TILES, E])
        wexp_h = sb("wexp_h", [P, NE, 6, P], F32R)
        wexp_l = sb("wexp_l", [P, NE, 6, P], F32R)
        id_s = sb("id_s", [P, P])
        idb_s = sb("idb_s", [P, SPAN], BF16)
        causal_s = sb("causal_s", [P, HG, N], BF16)
        hmask_s = sb("hmask_s", [P, HG])
        vmask_s = sb("vmask_s", [2 * N, 2])
        below_s = sb("below_s", [P, E, E], BF16)
        half_s = sb("half_s", [P, 1])
        eps_s = sb("eps_s", [P, 1])
        shared_s = sb("shared_s", [P, 1])
        x_s = sb("x_s", [P, PC, TOK])
        h_nat = sb("h_nat", [P, TILES, D])
        xn = sb("xn", [P, TILES, D])
        t_h = sb("t_h", [P, 2, TOK], F32R)
        t_l = sb("t_l", [P, 2, TOK], F32R)
        turn = sb("turn", [P, 4 * TOK])
        tT = turn[:, 0:2 * TOK].rearrange("p (c t) -> p c t", c=2)
        v_sb = turn[0:2 * N, 0:PAIRS * D].rearrange("p (m d) -> p m d", d=D)
        combT = turn[0:E, 0:TOK]
        yo = turn[:, 2 * TOK:4 * TOK].rearrange("p (c t) -> p c t", c=2)
        st = sb("st", [P, 2, TILES, 6])
        mv = sb("mv", [P, 2, TILES, 2])
        ve = sb("ve", [P, 2, TILES])
        rstd = sb("rstd", [P, 2, TILES])
        qT = sb("qT", [P, 2, IMGS, N])
        kT = sb("kT", [P, 2, IMGS, N])
        work = sb("work", [P, 4 * HG * N + 2 * HEADS * N])
        bdk = work[:, 0:4 * HG * N].rearrange("p (g m n) -> p g m n", g=2, m=2)
        ex = work[:, 4 * HG * N:].rearrange("p (b h k) -> p b h k", b=2, h=HEADS)
        w_raw = work[:, 0:8 * D].rearrange("p (n c d) -> p n c d", n=4, c=2)
        below_f = turn[:, HG * N:HG * N + E * E].rearrange("p (e f) -> p e f", e=E)
        causal_f = turn[:, 0:HG * N].rearrange("p (h k) -> p h k", h=HG)
        tmp = sb("tmp", [P, 12 * P])
        th, s1, us, gs = (tmp[:, TOK * n:TOK * n + TOK] for n in range(4))
        bdv = sb("bdv", [2 * N, IMGS, D])
        nmax = sb("nmax", [P, 2, HEADS])
        rsum = sb("rsum", [P, 2, HEADS])
        rinv = sb("rinv", [P, 2, HEADS])
        ptT = sb("ptT", [2 * N, 8, 2, N])
        lg = sb("lg", [P, TILES, E])
        sc = sb("sc", [P, TILES, E])
        biased = sb("biased", [P, TILES, E])
        gmax = sb("gmax", [P, TILES, GROUPS])
        gcmp = sb("gcmp", [P, 2, TILES, GROUPS, GROUPS], BF16)
        ecmp = work[:, 0:TILES * E * E].bitcast(BF16).rearrange("p (s t e f) -> p s t e f", s=2, t=TILES, e=E)
        grank = sb("grank", [P, TILES, GROUPS])
        keep = sb("keep", [P, TILES, GROUPS])
        kneg = sb("kneg", [P, TILES, GROUPS])
        sm = sb("sm", [P, TILES, E])
        rank = sb("rank", [P, TILES, E])
        comb = sb("comb", [P, TILES, E])
        x_h = sb("x_h", [P, 2, 2, TOK], F32R)
        x_l = sb("x_l", [P, 2, 2, TOK], F32R)
        h2T = sb("h2T", [P, 2, 2, TOK])
        cb = sb("cb", [P, 2, 2, TOK])
        raw = [a.rearrange("p (c q) -> p c q", c=6) for a in
               (tmp[:, 0:6 * P], tmp[:, 6 * P:12 * P], cb[:].rearrange("p b e t -> p (b e t)")[:, 0:6 * P])]
        SLOTS = len(raw)
        g_h = sb("g_h", [P, 2, TOK], F32R)
        g_l = sb("g_l", [P, 2, TOK], F32R)

        front = [ctx.enter_context(nc.psum_tensor(f"front{b}", [P, 512], F32)) for b in range(4)]
        ps_h1, ps_h3, ps_y0, ps_y1 = (ctx.enter_context(nc.psum_tensor(n, [P, 512], F32))
                                      for n in ("ps_h1", "ps_h3", "ps_y0", "ps_y1"))

        names = """fills x_first x_in w_in raw_in0 raw_in1 raw_in2 raw_h raw_l tab_sum init
        banks_zero wp_in table_in w_h_ok wqk_l_ok wvo_l_ok patched h_ok h_stat h_agg h_var h_rstd
        xn_ok xT_ps th_h_ok th_l_ok qk_ps qk_ok v_ps v_ok v_in bdv_ok
        bdk0 bdk1 s_ps s_max s_sub s_exp s_sum s_inv s_norm pt_ps pt_ok o_ps oh_ok o_ok
        wo_ps h2_ok h2_stat h2_agg h2_var h2_rstd x2_ok t2_ps t2_ok xh_ok xl_ok lg_ps lg_exp
        route_step ct_ps ct_ok cb_stored cb_in0 cb_in1
        h1_ps h3_ps th_ok s1_ok u_ok y_out g_ok gh_ok gl_ok y_ps yo_ok stored""".split()
        S = {n: ctx.enter_context(nc.semaphore(n)) for n in names}
        block = ctx.enter_context(nc.Block())
        TABLE_LOADS = 3
        CONST_LOADS = 7
        FILLS = 3
        INITS = 4
        ROUTE_STEPS = 18
        PATCH_BANKS = (2, 3, 0)
        TURN_BANKS = (2, 3, 0)

        def tile(t):
            return slice(P * t, P * t + ROWS[t])

        def turned1(t):
            return front[TURN_BANKS[t]][:, 0:2 * P].rearrange("p (c t) -> p c t", c=2)

        def turned2(t):
            return front[TURN_BANKS[t]][:].rearrange("p (c t) -> p c t", c=4)

        def parity(buf, i):
            return buf[:, bass.ds(i % 2, 1)].rearrange("p b c t -> p (b c) t")

        def passes(slot):
            before = 0
            for name, n in FILL.items():
                if name == slot:
                    return range(before - 1, before - 1 + n)
                before += n
            return range(0)

        @block.sync
        def _(sp):
            sp.dma_start(wp_s[:], wpT).then_inc(S["wp_in"], 16)
            for dst, src in ((tab[:], pos), (h_nat[:], bias), (id_s[:], ident)):
                sp.dma_start(dst, src).then_inc(S["table_in"], 16)
            for dst, src in ((w_raw, wqkvo), (causal_f, causal), (hmask_s[:], hmask), (vmask_s[:], vmask),
                             (gate_s[:], gateT), (gb_s[:], gbias), (below_f, below)):
                sp.dma_start(dst, src).then_inc(S["w_in"], 16)

            def load_experts(es):
                for e in es:
                    if e >= SLOTS:
                        sp.wait_ge(S["raw_l"], e - SLOTS + 1)
                    sp.dma_start(raw[e % SLOTS], wexp[:, e]).then_inc(S[f"raw_in{e % SLOTS}"], 16)

            def values(i):
                sp.wait_ge(S["v_ok"], (i + 1) * PAIRS)
                for r in range(2):
                    for im in range(2):
                        sp.dma_start(bdv[N * r:N * r + N].rearrange("t (p m) d -> t p m d", m=2)[:, :, im],
                                     v_sb[N * im:N * im + N]).then_inc(S["v_in"], 16)

            def next_images(i):
                sp.wait_ge(S["patched"], (i + 1) * TILES)
                sp.dma_start(x_s[:], xT[bass.ds(i + 1, 1)].rearrange("i p c t -> p (i c) t")) \
                    .then_inc(S["x_in"], 16)

            def weights_rows(i, first):
                sp.wait_ge(S["ct_ok"], i + 1)
                sp.dma_start(comb_dram[bass.ds(i, 1)].rearrange("i e t -> (i e) t"), combT) \
                    .then_inc(S["cb_stored"], 16)
                if not first:
                    sp.wait_ge(S["yo_ok"], i)
                    sp.dma_start(out[:, :, bass.ds((i - 1) * TOK, TOK)], yo).then_inc(S["stored"], 16)
                sp.wait_ge(S["cb_stored"], (i + 1) * 16)

            def spread(i, q, first):
                if q >= 2:
                    sp.wait_ge(S["g_ok"], i * NE + 2 * q - 1)
                elif not first:
                    sp.wait_ge(S["g_ok"], (i - 1) * NE + NE - 2 + 2 * q)
                src = comb_dram[bass.ds(i, 1), 2 * q:2 * q + 2].rearrange("i e t -> i (e t)")
                sp.dma_start(cb[:, q % 2].rearrange("p e t -> p (e t)"), src.to_broadcast([P, 2 * TOK])) \
                    .then_inc(S[f"cb_in{q % 2}"], 16)

            def iteration(i, first, more):
                weights_rows(i, first)
                for q in range(2):
                    spread(i, q, first)
                values(i + 1)
                if more:
                    next_images(i + 1)
                for q in range(2, E // 2):
                    spread(i, q, first)

            sp.sem_inc(S["stored"], 16)
            load_experts(range(SLOTS + 2))
            values(0)
            load_experts(range(SLOTS + 2, 2 * SLOTS))
            next_images(0)
            load_experts(range(2 * SLOTS, NE))
            sp.wait_ge(S["raw_l"], NE)
            iteration(0, True, True)
            with sp.Fori(1, ITERS - 2) as i:
                iteration(i, False, True)
            iteration(ITERS - 2, False, False)
            weights_rows(ITERS - 1, False)
            for q in range(E // 2):
                spread(ITERS - 1, q, False)
            for slot in range(2):
                sp.wait_ge(S[f"cb_in{slot}"], 16 * ITERS * E // 4)
            sp.wait_ge(S["yo_ok"], ITERS)
            sp.dma_start(out[:, :, (ITERS - 1) * TOK:ITERS * TOK], yo).then_inc(S["stored"], 16)
            sp.wait_ge(S["stored"], 16 * (ITERS + 1))

        @block.gpsimd
        def _(pool):
            pool.memset(half_s[:], -0.5).then_inc(S["fills"], 1)
            pool.memset(eps_s[:], EPS).then_inc(S["fills"], 1)
            pool.memset(shared_s[:], 0.5).then_inc(S["fills"], 1)
            pool.wait_ge(S["fills"], FILLS)

            def weigh(j, k):
                pool.wait_ge(S["u_ok"], j * NE + k + 1)
                if k >= 1:
                    q = (k - 1) // 2
                    pool.wait_ge(S[f"cb_in{q % 2}"], 16 * (j * (E // 4) + q // 2 + 1))
                if k >= 1:
                    pool.wait_ge(S["gl_ok"], j * NE + k)
                weights = cb[:, (k - 1) // 2 % 2, (k - 1) % 2] if k else shared_s[:].to_broadcast([P, TOK])
                pool.tensor_tensor(gs, us, weights, ALU.mult).then_inc(S["g_ok"], 1)

            def experts(j, slot):
                if j is None:
                    for e in SPLIT.get(slot, ()):
                        pool.wait_ge(S["raw_h"], e + 1)
                        pool.tensor_tensor(wexp_l[:, e], raw[e % SLOTS], wexp_h[:, e].bitcast(F32),
                                           ALU.subtract).then_inc(S["raw_l"], 1)
                else:
                    for k in passes(slot):
                        if k + 1 < NE:
                            weigh(j, k + 1)
                    if slot == "route2":
                        pool.wait_ge(S["y_out"], j + 1)
                        pool.tensor_tensor(yo, yo, parity(h2T, j), ALU.add).then_inc(S["yo_ok"], 1)

            def rstds(i, which, tiles, agg, var, done):
                for t in tiles:
                    r = ROWS[t]
                    pool.wait_ge(S[agg], i * TILES + t + 1)
                    pool.tensor_tensor(ve[0:r, which, t:t + 1], mv[0:r, which, t, 1:2], eps_s[0:r],
                                       ALU.add).then_inc(S[var], 1)
                    pool.wait_ge(S[var], i * TILES + t + 1)
                    pool.tensor_tensor(rstd[0:r, which, t:t + 1], ve[0:r, which, t:t + 1], half_s[0:r],
                                       ALU.pow).then_inc(S[done], 1)

            def iteration(i, j, more):
                for slot in ("norm1", "turn1"):
                    experts(j, slot)

                def heads_apart(p):
                    if p == 0:
                        pool.wait_ge(S["qk_ok"], i * 4 + 4)
                    else:
                        pool.wait_ge(S["s_ps"], i * PAIRS + p)
                    pool.tensor_tensor(
                        bdk[:, 1].rearrange("p m (h k) -> p m h k", h=HG),
                        kT[:, 1, 2 * p:2 * p + 2, None, :].to_broadcast([P, 2, HG, N]),
                        hmask_s[:, None, :, None].to_broadcast([P, 2, HG, N]),
                        ALU.mult).then_inc(S["bdk1"], 1)

                heads_apart(0)
                experts(j, "v")
                for p in range(PAIRS + 1):
                    if p + 1 < PAIRS:
                        heads_apart(p + 1)
                    experts(j, f"att{p}a")
                    if p < PAIRS:
                        pool.wait_ge(S["s_inv"], i * PAIRS + p + 1)
                        pool.tensor_tensor(ex[0:SPAN, p % 2], ex[0:SPAN, p % 2],
                                           rinv[0:SPAN, p % 2, :, None].to_broadcast([SPAN, HEADS, N]),
                                           ALU.mult).then_inc(S["s_norm"], 1)
                    experts(j, f"att{p}b")
                experts(j, "wo")
                rstds(i, 1, range(TILES), "h2_agg", "h2_var", "h2_rstd")
                for slot in ("norm2", "turn2", "route0", "route1"):
                    experts(j, slot)
                if more:
                    rstds(i + 1, 0, range(2), "h_agg", "h_var", "h_rstd")
                experts(j, "route2")
                experts(i, "next")
                if more:
                    rstds(i + 1, 0, range(2, TILES), "h_agg", "h_var", "h_rstd")

            def split_weight(n):
                pool.wait_ge(S["w_h_ok"], n + 1)
                pool.tensor_tensor(w_l[:, n], w_raw[:, n], w_h[:, n].bitcast(F32),
                                   ALU.subtract).then_inc(S["wvo_l_ok"], 1)

            rstds(0, 0, range(2), "h_agg", "h_var", "h_rstd")
            split_weight(2)
            rstds(0, 0, range(2, TILES), "h_agg", "h_var", "h_rstd")
            split_weight(3)
            pool.wait_ge(S["w_in"], 16 * CONST_LOADS)
            iteration(0, None, True)
            with pool.Fori(1, ITERS - 1) as i:
                iteration(i, i - 1, True)
            iteration(ITERS - 1, ITERS - 2, False)
            for slot in list(FILL)[1:]:
                experts(ITERS - 1, slot)

        @block.scalar
        def _(act):
            act.dma_start(x_s[:, :, 0:P], xT[0, :, :, 0:P]).then_inc(S["x_first"], 16)
            act.dma_start(x_s[:, :, P:TOK], xT[0, :, :, P:TOK]).then_inc(S["x_in"], 16)

            def experts(j, slot):
                if j is None:
                    for e in SPLIT.get(slot, ()):
                        act.wait_ge(S[f"raw_in{e % SLOTS}"], 16 * (e // SLOTS + 1))
                        act.activation(wexp_h[:, e], raw[e % SLOTS], ACT.Copy).then_inc(S["raw_h"], 1)
                else:
                    for k in passes(slot):
                        if k + 1 < NE:
                            act.wait_ge(S["h1_ps"], j * NE + k + 2)
                            if k >= 0:
                                act.wait_ge(S["s1_ok"], j * NE + k + 1)
                            act.activation(th, ps_h1[:, 0:TOK], ACT.Tanh, scale=0.5).then_inc(S["th_ok"], 1)
                        if 0 <= k < NE:
                            act.wait_ge(S["g_ok"], j * NE + k + 1)
                            if k >= 2:
                                act.wait_ge(S["y_ps"], j * NE + k - 1)
                            act.activation(g_h[:, k % 2], gs, ACT.Copy).then_inc(S["gh_ok"], 1)
                    if slot == "route2":
                        act.wait_ge(S["y_ps"], (j + 1) * NE)
                        act.wait_ge(S["stored"], 16 * (j + 1))
                        act.activation(yo[:, 0], ps_y0[:, 0:TOK], ACT.Copy)
                        act.activation(yo[:, 1], ps_y1[:, 0:TOK], ACT.Copy).then_inc(S["y_out"], 1)

            def iteration(i, j):
                experts(j, "norm1")
                for t in range(TILES):
                    act.wait_ge(S["xT_ps"], i * TILES + t + 1)
                    act.activation(t_h[:, :, tile(t)], turned1(t)[:, :, 0:ROWS[t]],
                                   ACT.Copy).then_inc(S["th_h_ok"], 1)
                experts(j, "turn1")
                for n in range(4):
                    g, is_k = divmod(n, 2)
                    act.wait_ge(S["qk_ps"], i * 4 + n + 1)
                    act.activation((kT if is_k else qT)[:, g], front[n][:, 0:TOK].rearrange("p (m t) -> p m t", t=N),
                                   ACT.Copy, scale=1.0 if is_k else HD ** -0.5).then_inc(S["qk_ok"], 1)
                for p in range(PAIRS):
                    if p == 0 and j is not None:
                        act.wait_ge(S["cb_stored"], 16 * i)
                        act.wait_ge(S["stored"], 16 * (j + 1))
                    act.wait_ge(S["v_ps"], i * PAIRS + p + 1)
                    act.activation(v_sb[:, p], front[p][0:2 * N, 0:D], ACT.Copy).then_inc(S["v_ok"], 1)
                experts(j, "v")
                def exponentials(p):
                    act.wait_ge(S["s_sub"], i * PAIRS + p + 1)
                    act.activation(ex[0:SPAN, p % 2], ex[0:SPAN, p % 2], ACT.Exp).then_inc(S["s_exp"], 1)

                def probabilities(q):
                    for hf in range(2):
                        act.wait_ge(S["pt_ps"], (i * PAIRS + q) * 2 + hf + 1)
                        act.activation(
                            ptT[:, 4 * hf:4 * hf + 4],
                            front[2 + hf][0:2 * N, :].rearrange("p (c m t) -> p c m t", c=4, m=2)[:, :, :, 0:N],
                            ACT.Copy).then_inc(S["pt_ok"], 1)

                for p in range(PAIRS + 1):
                    q = p - 1
                    experts(j, f"att{p}a")
                    if j is not None and p < PAIRS:
                        exponentials(p)
                    if p >= 1:
                        probabilities(q)
                    if j is None and p < PAIRS:
                        exponentials(p)
                    if p < PAIRS:
                        act.wait_ge(S["v_in"], (i + 1) * 64)
                        for odd in range(2):
                            vals = bdv[:, 2 * p:2 * p + 2].rearrange("t m (g o d) -> t (m g) o d", o=2, d=HD)
                            act.activation(vals[:, :, odd], vals[:, :, odd], ACT.Copy,
                                           scale=vmask_s[:, odd:odd + 1]).then_inc(S["bdv_ok"], 1)
                    if j is not None:
                        experts(j, f"att{p}b")
                    if p >= 1:
                        act.wait_ge(S["o_ps"], i * PAIRS + q + 1)
                        act.activation(t_h[:, :, 2 * N * q:2 * N * (q + 1)],
                                       front[2][:, 0:4 * N].rearrange("p (g t) -> p g t", g=2),
                                       ACT.Copy).then_inc(S["oh_ok"], 1)
                    if j is None:
                        experts(j, f"att{p}b")
                experts(j, "wo")
                experts(j, "norm2")
                for t in range(TILES):
                    act.wait_ge(S["t2_ps"], i * TILES + t + 1)
                    turned = turned2(t)[:, :, 0:ROWS[t]]
                    act.activation(tT[:, :, tile(t)], turned[:, 2:4], ACT.Copy).then_inc(S["t2_ok"], 1)
                    act.activation(parity(h2T, i)[:, :, tile(t)], turned[:, 0:2], ACT.Copy).then_inc(S["t2_ok"], 1)
                act.wait_ge(S["w_in"], 16 * CONST_LOADS)
                act.wait_ge(S["t2_ok"], (i + 1) * TILES * 2)
                act.activation(parity(x_h, i), tT, ACT.Copy).then_inc(S["xh_ok"], 1)
                experts(j, "turn2")
                act.wait_ge(S["lg_ps"], i + 1)
                act.activation(lg[:], front[1][:, 0:TILES * E].rearrange("p (t e) -> p t e", e=E), ACT.Exp,
                               scale=-1.0).then_inc(S["lg_exp"], 1)
                for slot in ("route0", "route1", "route2"):
                    experts(j, slot)
                if j is None:
                    act.wait_ge(S["raw_l"], NE)
                experts(i, "next")
                act.wait_ge(S["ct_ps"], i + 1)
                act.activation(combT, front[1][0:E, 0:TOK], ACT.Copy).then_inc(S["ct_ok"], 1)

            act.wait_ge(S["w_in"], 16 * CONST_LOADS)
            for n in range(4):
                act.activation(w_h[:, n], w_raw[:, n], ACT.Copy).then_inc(S["w_h_ok"], 1)
            iteration(0, None)
            with act.Fori(1, ITERS) as i:
                iteration(i, i - 1)
            for slot in list(FILL)[1:]:
                experts(ITERS - 1, slot)

        @block.vector
        def _(dve):
            for b in front:
                dve.memset(b[:], 0.0).then_inc(S["banks_zero"], 1)
            dve.memset(xn[:], 0.0).then_inc(S["init"], 1)
            dve.wait_ge(S["table_in"], 16 * TABLE_LOADS)
            dve.tensor_tensor(tab[:], tab[:], h_nat[:], ALU.add).then_inc(S["tab_sum"], 1)
            dve.wait_ge(S["tab_sum"], 1)

            def experts(j, slot):
                if j is None:
                    return
                for k in passes(slot):
                    if k + 1 < NE:
                        dve.wait_ge(S["th_ok"], j * NE + k + 2)
                        if k >= 0:
                            dve.wait_ge(S["u_ok"], j * NE + k + 1)
                        dve.scalar_tensor_tensor(s1, th, 1.0, ps_h1[:, 0:TOK], ALU.add,
                                                 ALU.mult).then_inc(S["s1_ok"], 1)
                    if 0 <= k < NE:
                        dve.wait_ge(S["gh_ok"], j * NE + k + 1)
                        if k >= 2:
                            dve.wait_ge(S["y_ps"], j * NE + k - 1)
                        dve.tensor_tensor(g_l[:, k % 2], gs, g_h[:, k % 2].bitcast(F32),
                                          ALU.subtract).then_inc(S["gl_ok"], 1)
                    if k + 1 < NE:
                        dve.wait_ge(S["s1_ok"], j * NE + k + 2)
                        dve.wait_ge(S["h3_ps"], j * NE + k + 2)
                        if k >= 0:
                            dve.wait_ge(S["g_ok"], j * NE + k + 1)
                        dve.tensor_tensor(us, s1, ps_h3[:, 0:TOK],
                                          ALU.mult).then_inc(S["u_ok"], 1)

            def norm_stats(i, t, which, bank, ps, other, res, pre):
                r = ROWS[t]
                dve.wait_ge(S[ps], i * TILES + t + 1)
                dve.tensor_tensor(res[0:r, t], front[bank][0:r, 0:D], other[0:r, t],
                                  ALU.add).then_inc(S[pre + "_ok"], 1)
                dve.wait_ge(S[pre + "_ok"], i * TILES + t + 1)
                dve.bn_stats(st[0:r, which, t], res[0:r, t]).then_inc(S[pre + "_stat"], 1)
                dve.wait_ge(S["table_in"], 16 * TABLE_LOADS)
                dve.wait_ge(S[pre + "_stat"], i * TILES + t + 1)
                dve.bn_aggr(mv[0:r, which, t], st[0:r, which, t]).then_inc(S[pre + "_agg"], 1)

            def norm_apply(i, which, res, pre, done):
                for t in range(TILES):
                    r = ROWS[t]
                    dve.wait_ge(S[pre + "_agg"], i * TILES + t + 1)
                    dve.wait_ge(S[pre + "_rstd"], i * TILES + t + 1)
                    dve.tensor_scalar(xn[0:r, t], res[0:r, t], mv[0:r, which, t, 0:1],
                                      rstd[0:r, which, t:t + 1], ALU.subtract, ALU.mult).then_inc(S[done], 1)

            def embed_stats(i, t):
                norm_stats(i, t, 0, PATCH_BANKS[t], "patched", tab, h_nat, "h")

            def embed_apply(i):
                norm_apply(i, 0, h_nat, "h", "xn_ok")

            def iteration(i, j, more):
                for t in range(TILES):
                    dve.wait_ge(S["th_h_ok"], i * TILES + t + 1)
                    dve.tensor_tensor(t_l[:, :, tile(t)], turned1(t)[:, :, 0:ROWS[t]],
                                      t_h[:, :, tile(t)].bitcast(F32), ALU.subtract).then_inc(S["th_l_ok"], 1)
                experts(j, "norm1")
                experts(j, "turn1")

                def heads_apart(p):
                    if p == 0:
                        dve.wait_ge(S["qk_ok"], i * 4 + 4)
                    if p >= 1:
                        dve.wait_ge(S["s_ps"], i * PAIRS + p)
                    dve.tensor_tensor(
                        bdk[:, 0].rearrange("p m (h k) -> p m h k", h=HG),
                        kT[:, 0, 2 * p:2 * p + 2, None, :].to_broadcast([P, 2, HG, N]),
                        hmask_s[:, None, :, None].to_broadcast([P, 2, HG, N]),
                        ALU.mult).then_inc(S["bdk0"], 1)

                heads_apart(0)
                experts(j, "v")
                for p in range(PAIRS + 1):
                    if p < PAIRS:
                        dve.wait_ge(S["s_ps"], i * PAIRS + p + 1)
                        for g in range(2):
                            a = dve.tensor_reduce(nmax[0:SPAN, p % 2, HG * g:HG * g + HG],
                                                  front[g][0:SPAN, 0:HG * N].rearrange("p (h k) -> p h k", h=HG),
                                                  AX.X, ALU.max, negate=True)
                        a.then_inc(S["s_max"], 1)
                        dve.wait_ge(S["s_max"], i * PAIRS + p + 1)
                        if p >= 2:
                            dve.wait_ge(S["pt_ps"], (i * PAIRS + p - 1) * 2)
                        for g in range(2):
                            a = dve.tensor_tensor(
                                ex[0:SPAN, p % 2, HG * g:HG * g + HG],
                                front[g][0:SPAN, 0:HG * N].rearrange("p (h k) -> p h k", h=HG),
                                nmax[0:SPAN, p % 2, HG * g:HG * g + HG, None].to_broadcast([SPAN, HG, N]), ALU.add)
                        a.then_inc(S["s_sub"], 1)
                    experts(j, f"att{p}a")
                    if p + 1 < PAIRS:
                        heads_apart(p + 1)
                    if p < PAIRS:
                        dve.wait_ge(S["s_exp"], i * PAIRS + p + 1)
                        dve.tensor_reduce(rsum[0:SPAN, p % 2], ex[0:SPAN, p % 2], AX.X,
                                          ALU.add).then_inc(S["s_sum"], 1)
                        dve.wait_ge(S["s_sum"], i * PAIRS + p + 1)
                        dve.reciprocal(rinv[0:SPAN, p % 2], rsum[0:SPAN, p % 2]).then_inc(S["s_inv"], 1)
                    experts(j, f"att{p}b")
                    if p >= 1:
                        q = p - 1
                        dve.wait_ge(S["oh_ok"], i * PAIRS + q + 1)
                        cols = slice(2 * N * q, 2 * N * (q + 1))
                        dve.tensor_tensor(t_l[:, :, cols], front[2][:, 0:4 * N].rearrange("p (g t) -> p g t", g=2),
                                          t_h[:, :, cols].bitcast(F32), ALU.subtract).then_inc(S["o_ok"], 1)
                experts(j, "wo")
                for t in range(TILES):
                    norm_stats(i, t, 1, t % 2, "wo_ps", h_nat, h_nat, "h2")
                norm_apply(i, 1, h_nat, "h2", "x2_ok")
                experts(j, "norm2")
                dve.wait_ge(S["w_in"], 16 * CONST_LOADS)
                dve.wait_ge(S["xh_ok"], i + 1)
                dve.tensor_tensor(parity(x_l, i), tT, parity(x_h, i).bitcast(F32),
                                  ALU.subtract).then_inc(S["xl_ok"], 1)
                experts(j, "turn2")

                r = i * ROUTE_STEPS
                dve.wait_ge(S["lg_exp"], i + 1)
                dve.tensor_scalar(lg[:], lg[:], 1.0, None, ALU.add).then_inc(S["route_step"], 1)
                dve.wait_ge(S["route_step"], r + 1)
                dve.reciprocal(sc[:], lg[:]).then_inc(S["route_step"], 1)
                dve.wait_ge(S["route_step"], r + 2)
                dve.tensor_tensor(biased[:], sc[:], gb_s[:], ALU.add).then_inc(S["route_step"], 1)
                dve.wait_ge(S["route_step"], r + 3)
                by_group = biased[:].rearrange("p t (g k) -> p (t g) k", g=GROUPS)
                dve.tensor_reduce(gmax[:].rearrange("p t g -> p (t g)"), by_group, AX.X,
                                  ALU.max).then_inc(S["route_step"], 1)
                dve.wait_ge(S["route_step"], r + 4)
                mine = gmax[:, :, :, None].to_broadcast([P, TILES, GROUPS, GROUPS])
                other = gmax[:, :, None, :].to_broadcast([P, TILES, GROUPS, GROUPS])
                lower = below_s[:, None, 0:GROUPS, 0:GROUPS].to_broadcast([P, TILES, GROUPS, GROUPS])
                dve.tensor_tensor(gcmp[:, 0], other, mine, ALU.is_gt)
                dve.tensor_tensor(gcmp[:, 1], other, mine, ALU.is_equal).then_inc(S["route_step"], 1)
                dve.wait_ge(S["route_step"], r + 5)
                dve.tensor_tensor(gcmp[:, 1], gcmp[:, 1], lower, ALU.mult).then_inc(S["route_step"], 1)
                dve.wait_ge(S["route_step"], r + 6)
                dve.tensor_tensor(gcmp[:, 0], gcmp[:, 0], gcmp[:, 1], ALU.add).then_inc(S["route_step"], 1)
                dve.wait_ge(S["route_step"], r + 7)
                dve.tensor_reduce(grank[:], gcmp[:, 0], AX.X, ALU.add).then_inc(S["route_step"], 1)
                dve.wait_ge(S["route_step"], r + 8)
                if j is not None and more:
                    embed_stats(i + 1, 0)
                experts(j, "route0")
                dve.tensor_scalar(keep[:], grank[:], float(TOPG), None, ALU.is_lt).then_inc(S["route_step"], 1)
                dve.wait_ge(S["route_step"], r + 9)
                dve.tensor_scalar(kneg[:], keep[:], -1.0, -NEG, ALU.add, ALU.mult).then_inc(S["route_step"], 1)
                dve.wait_ge(S["route_step"], r + 10)
                masked = sm[:].rearrange("p t (g k) -> p (t g) k", g=GROUPS)
                shape = [P, TILES * GROUPS, E // GROUPS]
                dve.tensor_tensor(masked, by_group,
                                  keep[:].rearrange("p t g -> p (t g)")[:, :, None].to_broadcast(shape),
                                  ALU.mult).then_inc(S["route_step"], 1)
                dve.wait_ge(S["route_step"], r + 11)
                dve.tensor_tensor(masked, masked,
                                  kneg[:].rearrange("p t g -> p (t g)")[:, :, None].to_broadcast(shape),
                                  ALU.add).then_inc(S["route_step"], 1)
                dve.wait_ge(S["route_step"], r + 12)
                experts(j, "route1")
                mine = sm[:, :, :, None].to_broadcast([P, TILES, E, E])
                other = sm[:, :, None, :].to_broadcast([P, TILES, E, E])
                lower = below_s[:, None, 0:E, 0:E].to_broadcast([P, TILES, E, E])
                dve.tensor_tensor(ecmp[:, 0], other, mine, ALU.is_gt)
                dve.tensor_tensor(ecmp[:, 1], other, mine, ALU.is_equal).then_inc(S["route_step"], 1)
                dve.wait_ge(S["route_step"], r + 13)
                dve.tensor_tensor(ecmp[:, 1], ecmp[:, 1], lower, ALU.mult).then_inc(S["route_step"], 1)
                dve.wait_ge(S["route_step"], r + 14)
                if j is None:
                    embed_stats(i + 1, 0)
                if more:
                    embed_stats(i + 1, 1)
                dve.tensor_tensor(ecmp[:, 0], ecmp[:, 0], ecmp[:, 1], ALU.add).then_inc(S["route_step"], 1)
                dve.wait_ge(S["route_step"], r + 15)
                dve.tensor_reduce(rank[:], ecmp[:, 0], AX.X, ALU.add).then_inc(S["route_step"], 1)
                dve.wait_ge(S["route_step"], r + 16)
                dve.tensor_scalar(rank[:], rank[:], float(TOPK), 0.5, ALU.is_lt,
                                  ALU.mult).then_inc(S["route_step"], 1)
                dve.wait_ge(S["route_step"], r + 17)
                dve.tensor_tensor(comb[:], rank[:], sc[:], ALU.mult).then_inc(S["route_step"], 1)
                experts(j, "route2")
                experts(i, "next")
                if more:
                    embed_stats(i + 1, 2)
                    embed_apply(i + 1)

            for t in range(2):
                embed_stats(0, t)
            dve.wait_ge(S["w_in"], 16 * CONST_LOADS)
            dve.tensor_copy(idb_s[:], id_s[:, 0:SPAN]).then_inc(S["init"], 1)
            dve.tensor_copy(causal_s[:], causal_f).then_inc(S["init"], 1)
            dve.tensor_copy(below_s[:], below_f).then_inc(S["init"], 1)
            for n in range(2):
                dve.wait_ge(S["w_h_ok"], n + 1)
                dve.tensor_tensor(w_l[:, n], w_raw[:, n], w_h[:, n].bitcast(F32),
                                  ALU.subtract).then_inc(S["wqk_l_ok"], 1)
            embed_stats(0, 2)
            embed_apply(0)
            iteration(0, None, True)
            with dve.Fori(1, ITERS - 1) as i:
                iteration(i, i - 1, True)
            iteration(ITERS - 1, ITERS - 2, False)
            for slot in list(FILL)[1:]:
                experts(ITERS - 1, slot)

        @block.tensor
        def _(pe):
            def patch(t):
                for c in range(PC):
                    m = pe.matmul(front[PATCH_BANKS[t]][0:ROWS[t], 0:D], x_s[:, c, tile(t)], wp_s[:, c],
                                  start=(c == 0), stop=(c == PC - 1))
                m.then_inc(S["patched"], 1)

            pe.wait_ge(S["banks_zero"], len(front))
            pe.wait_ge(S["x_first"], 16)
            pe.wait_ge(S["wp_in"], 16)
            patch(0)
            pe.wait_ge(S["x_in"], 16)
            for t in range(1, TILES):
                patch(t)
            pe.wait_ge(S["w_in"], 16 * CONST_LOADS)
            pe.wait_ge(S["init"], INITS)

            def split_product(o, stat_h, stat_l, mov_h, mov_l, first, last):
                pe.matmul(o, stat_h, mov_h, start=first, stop=False)
                pe.matmul(o, stat_h, mov_l, start=False, stop=False)
                return pe.matmul(o, stat_l, mov_h, start=False, stop=last)

            def up(j, k):
                for w, o in ((0, ps_h1), (1, ps_h3)):
                    if k >= 1 and w == 0:
                        pe.wait_ge(S["s1_ok"], j * NE + k)
                    if k >= 1 and w == 1:
                        pe.wait_ge(S["u_ok"], j * NE + k)
                    for d in range(2):
                        c = 2 * w + d
                        m = split_product(o[:, 0:TOK], wexp_h[:, k, c], wexp_l[:, k, c],
                                          parity(x_h, j)[:, d], parity(x_l, j)[:, d], d == 0, d == 1)
                    m.then_inc(S["h3_ps" if w else "h1_ps"], 1)

            def down(j, k):
                pe.wait_ge(S["gl_ok"], j * NE + k + 1)
                for d, o in ((0, ps_y0), (1, ps_y1)):
                    m = split_product(o[:, 0:TOK], wexp_h[:, k, 4 + d], wexp_l[:, k, 4 + d],
                                      g_h[:, k % 2], g_l[:, k % 2], k == 0, k == NE - 1)
                m.then_inc(S["y_ps"], 1)

            def experts(j, slot):
                if j is None:
                    return
                for k in passes(slot):
                    if k == -1:
                        pe.wait_ge(S["xl_ok"], j + 1)
                    if k + 1 < NE:
                        up(j, k + 1)
                    if 1 <= k <= NE:
                        down(j, k - 1)

            def iteration(i, j, more):
                experts(j, "norm1")
                for t in range(TILES):
                    pe.wait_ge(S["xn_ok"], i * TILES + t + 1)
                    for c in range(2):
                        m = pe.transpose(turned1(t)[:, c], xn[:, t, P * c:P * c + P], id_s[:])
                    m.then_inc(S["xT_ps"], 1)
                experts(j, "turn1")
                if j is None:
                    pe.wait_ge(S["wqk_l_ok"], 2)
                pe.wait_ge(S["th_l_ok"], (i + 1) * TILES)
                for n in range(4):
                    g, is_k = divmod(n, 2)
                    if n == 1 and j is not None:
                        pe.wait_ge(S["ct_ok"], i)
                    for c in range(2):
                        m = split_product(front[n][:, 0:TOK], w_h[:, is_k, c, P * g:P * g + P],
                                          w_l[:, is_k, c, P * g:P * g + P], t_h[:, c], t_l[:, c], c == 0, c == 1)
                    m.then_inc(S["qk_ps"], 1)
                if j is None:
                    pe.wait_ge(S["wvo_l_ok"], 2)
                for p in range(PAIRS):
                    pe.wait_ge(S["qk_ok"], i * 4 + p + 1)
                    for c in range(2):
                        cols = slice(2 * N * p, 2 * N * (p + 1))
                        m = split_product(front[p][0:2 * N, 0:D], t_h[:, c, cols], t_l[:, c, cols],
                                          w_h[:, 2, c], w_l[:, 2, c], c == 0, c == 1)
                    m.then_inc(S["v_ps"], 1)
                experts(j, "v")
                for p in range(PAIRS + 1):
                    if p < PAIRS:
                        pe.wait_ge(S["bdk0"], i * PAIRS + p + 1)
                        pe.wait_ge(S["bdk1"], i * PAIRS + p + 1)
                        if p == 0:
                            pe.wait_ge(S["v_ok"], (i + 1) * PAIRS)
                        else:
                            pe.wait_ge(S["s_sub"], i * PAIRS + p)
                        for g in range(2):
                            pe.matmul(front[g][0:SPAN, 0:HG * N], idb_s[:], causal_s[:].rearrange("k h q -> k (h q)"),
                                      start=True, stop=False)
                            for im in range(2):
                                m = pe.matmul(front[g][64 * im:64 * im + N, 0:HG * N], qT[:, g, 2 * p + im],
                                              bdk[:, g, im], start=False, stop=True)
                        m.then_inc(S["s_ps"], 1)
                    experts(j, f"att{p}a")
                    if p >= 1:
                        q = p - 1
                        pe.wait_ge(S["s_norm"], i * PAIRS + q + 1)
                        if q >= 1:
                            pe.wait_ge(S["o_ok"], i * PAIRS + q)
                        for hf in range(2):
                            for c in range(4):
                                h = 8 * hf + 2 * c
                                m = pe.transpose(front[2 + hf][0:2 * N, P * c:P * c + SPAN],
                                                 ex[0:SPAN, q % 2, h:h + 2].rearrange("p h k -> p (h k)"),
                                                 id_s[0:SPAN, 0:SPAN])
                            m.then_inc(S["pt_ps"], 1)
                    experts(j, f"att{p}b")
                    if p >= 1:
                        pe.wait_ge(S["bdv_ok"], (i * PAIRS + q + 1) * 2)
                        for hf in range(2):
                            pe.wait_ge(S["pt_ok"], (i * PAIRS + q) * 2 + hf + 1)
                            for im in range(2):
                                for c in range(4):
                                    col = 2 * N * hf + N * im
                                    m = pe.matmul(front[2][32 * c:32 * c + 32, col:col + N],
                                                  bdv[:, 2 * q + im, P * hf + 32 * c:P * hf + 32 * c + 32],
                                                  ptT[:, 4 * hf + c, im], start=True, stop=True)
                        m.then_inc(S["o_ps"], 1)
                experts(j, "wo")
                pe.wait_ge(S["o_ok"], (i + 1) * PAIRS)
                for t in range(TILES):
                    if t >= 2:
                        pe.wait_ge(S["h2_ok"], i * TILES + t - 1)
                    for c in range(2):
                        m = split_product(front[t % 2][0:ROWS[t], 0:D], t_h[:, c, tile(t)], t_l[:, c, tile(t)],
                                          w_h[:, 3, c], w_l[:, 3, c], c == 0, c == 1)
                    m.then_inc(S["wo_ps"], 1)
                experts(j, "norm2")
                for t in range(TILES):
                    pe.wait_ge(S["x2_ok"], i * TILES + t + 1)
                    for c in range(4):
                        src = h_nat if c < 2 else xn
                        m = pe.transpose(turned2(t)[:, c], src[:, t, P * (c % 2):P * (c % 2) + P],
                                         id_s[:])
                    m.then_inc(S["t2_ps"], 1)
                experts(j, "turn2")
                pe.wait_ge(S["t2_ok"], (i + 1) * TILES * 2)
                for t in range(TILES):
                    for c in range(2):
                        m = pe.matmul(front[1][0:ROWS[t], E * t:E * t + E], tT[:, c, tile(t)], gate_s[:, c],
                                      start=(c == 0), stop=(c == 1))
                m.then_inc(S["lg_ps"], 1)
                if more:
                    pe.wait_ge(S["x_in"], (i + 2) * 16)
                    patch(0)
                experts(j, "route0")
                if more:
                    patch(1)
                experts(j, "route1")
                if more:
                    patch(2)
                experts(j, "route2")
                experts(i, "next")
                pe.wait_ge(S["route_step"], (i + 1) * ROUTE_STEPS)
                for t in range(TILES):
                    m = pe.transpose(front[1][0:E, tile(t)], comb[0:ROWS[t], t], id_s[0:ROWS[t], 0:ROWS[t]])
                m.then_inc(S["ct_ps"], 1)

            iteration(0, None, True)
            with pe.Fori(1, ITERS - 1) as i:
                iteration(i, i - 1, True)
            iteration(ITERS - 1, ITERS - 2, False)
            for slot in list(FILL)[1:]:
                experts(ITERS - 1, slot)


def _lay_out(inp):
    def rows(a):
        return np.ascontiguousarray(a.reshape(-1, P, a.shape[-1]).transpose(1, 0, 2))

    def tiled(a):
        full = np.zeros((TILES * P, a.shape[-1]), a.dtype)
        full[:TOK] = a
        return np.ascontiguousarray(full.reshape(TILES, P, -1).transpose(1, 0, 2))

    x = inp["x"]
    G = x.shape[-1] // 16
    patches = x.reshape(B, 3, G, 16, G, 16).transpose(1, 3, 5, 0, 2, 4).reshape(PC * P, B, G * G)
    xT = np.zeros((PC * P, B, N), x.dtype)
    xT[:, :, 1:] = patches
    xT = xT.reshape(PC, P, ITERS, TOK).transpose(2, 1, 0, 3)
    pos = np.concatenate([inp["cls_tok"][0], inp["L0_tok_pos_embd"][0]])
    bias = np.zeros((N, D), x.dtype)
    bias[1:] = inp["L0_tok_b"]
    wqkvo = np.stack([rows(inp["L0_attn_" + n]) for n in ("Wq", "Wk", "Wv", "Wo")], axis=1)
    w1 = np.concatenate([inp["L0_ffn_ws1"][None], inp["L0_ffn_w1"]])
    w3 = np.concatenate([inp["L0_ffn_ws3"][None], inp["L0_ffn_w3"]])
    w2 = np.concatenate([inp["L0_ffn_ws2"][None], inp["L0_ffn_w2"]])
    up = np.stack([w1, w3], axis=1).reshape(NE, 2, P, 2, P).transpose(4, 0, 1, 3, 2).reshape(P, NE, 4, P)
    down = w2.transpose(2, 0, 1).reshape(P, NE, 2, P)
    ch = np.arange(D)
    causal = np.zeros((P, N))
    causal[:N] = causal[64:SPAN] = np.where(np.arange(N)[None, :] > np.arange(N)[:, None], NEG, 0.0)
    return {
        "xT": xT, "wpT": rows(inp["L0_tok_W"].T), "pos": tiled(np.tile(pos, (IMGS, 1))),
        "bias": tiled(np.tile(bias, (IMGS, 1))), "wqkvo": wqkvo, "gateT": rows(inp["L0_ffn_gate_w"].T),
        "gbias": np.broadcast_to(inp["L0_ffn_gate_bias"], (P, TILES, E)), "wexp": np.concatenate([up, down], axis=2),
        "ident": np.eye(P, dtype=np.float32),
        "causal": np.repeat(causal[:, None], HG, axis=1).astype(np.float32),
        "hmask": (np.arange(P)[:, None] // HD == np.arange(HG)).astype(np.float32),
        "vmask": (np.arange(2 * N)[:, None] // N == np.arange(2)).astype(np.float32),
        "below": np.broadcast_to(np.tri(E, k=-1, dtype=np.float32), (P, E, E)),
    }


def kernel(**inputs):
    import concourse.bacc as _bacc
    from concourse.bass_utils import run_bass_kernel_spmd as _run

    nc = _bacc.Bacc("TRN2", target_bir_lowering=False, num_devices=1)
    laid = _lay_out({k: np.asarray(v) for k, v in inputs.items()})
    arrays, args = {}, []
    for name, a in laid.items():
        a = np.ascontiguousarray(a)
        arrays[f"in_{name}_dram"] = a
        args.append(nc.dram_tensor(f"in_{name}_dram", a.shape, mybir.dt.from_np(a.dtype), kind="ExternalInput").ap())
    args.append(nc.dram_tensor("out_dram", (P, 2, B * N), F32, kind="ExternalOutput").ap())
    args.append(nc.dram_tensor("token_weights", (ITERS, E, TOK), F32, kind="Internal").ap())
    build(nc, *args)
    r = _run(nc, [arrays], core_ids=[0])
    got = r.results[0]["out_dram"]
    return np.ascontiguousarray(got.transpose(2, 1, 0)).reshape(B, N, D)
```
